# Optimizing a Trainium2 kernel written in Bass

```python
import numpy as np
import jax
import jax.numpy as jnp

def _softmax(x, axis=-1):
    return jax.nn.softmax(x, axis=axis)

def _gelu(x):
    return jax.nn.gelu(x, approximate=True)

def _silu(x):
    return jax.nn.silu(x)

def _sigmoid(x):
    return jax.nn.sigmoid(x)

def _layernorm(x, axis=-1, eps=1e-05):
    m = jnp.mean(x, axis=axis, keepdims=True)
    v = jnp.var(x, axis=axis, keepdims=True)
    return (x - m) / jnp.sqrt(v + eps)

def _scatter_add(tgt, idx, src, axis=0):
    return tgt.at[idx].add(src)

def _segment_sum(src, seg, n):
    return jax.ops.segment_sum(src, seg, n)
kernel_name = 'mk_xattn_ffn_d1_seqx_r2_9a7529'

def setup_inputs(seed: int=0):
    np.random.seed(seed)
    _w = jnp.asarray

    def _rec_inputs():
        import jax
        import jax.numpy as jnp
        _rk = jax.random.key(seed)
        x = -0.0003929 + 0.9999 * jax.random.normal(jax.random.fold_in(_rk, 1), (4, 1024, 512), jnp.float32)
        _lenS = 1024 - jax.random.randint(jax.random.fold_in(_rk, 7), (4,), 0, max(1, 1024 // 4) + 1, jnp.int32)
        _lenS2 = 1024 - jax.random.randint(jax.random.fold_in(_rk, 8), (4,), 0, max(1, 1024 // 4) + 1, jnp.int32)
        _ctx_1024P = jax.random.normal(jax.random.fold_in(_rk, 11), (4, 16, 512), jnp.float32)
        _ctx_1024c = jax.random.dirichlet(jax.random.fold_in(_rk, 511), 0.3 * jnp.ones((16,), jnp.float32), (4, 1024))
        _ctx_1024t = jnp.einsum('bsk,bkd->bsd', _ctx_1024c, _ctx_1024P)
        _ctx_1024t = _ctx_1024t * jax.lax.rsqrt(jnp.mean(jnp.square(_ctx_1024t)) + 1e-12) * 0.953939
        ctx_1024 = 2.81802e-05 + 1.00001 * (_ctx_1024t + 0.3 * jax.random.normal(jax.random.fold_in(_rk, 611), (4, 1024, 512), jnp.float32))
        return (x, ctx_1024)
    x, ctx_1024 = _rec_inputs()

    def _L0_xattn_setup():
        import jax, jax.numpy as jnp
        import numpy as np
        B, L, D = (4, 2048, 512)
        key = jax.random.key(seed)
        k1, k2 = jax.random.split(key)
        Q = jax.random.normal(k1, (B, L, D), dtype=jnp.float32)
        K = jax.random.normal(k2, (B, L, D), dtype=jnp.float32)
        return {'Q': Q, 'K': K}
    _L0_xattn_all = _L0_xattn_setup()
    _L0_xattn_in = {k: v for k, v in _L0_xattn_all.items() if k in ()}
    del _L0_xattn_all

    def _L0_ffn_setup():
        import jax, jax.numpy as jnp
        import numpy as np
        IN_FEATURES = 512
        ACT_BITS = 4

        def _hadamard(size: int) -> np.ndarray:
            h = np.array([[1.0]], dtype=np.float64)
            while h.shape[0] < size:
                h = np.block([[h, h], [h, -h]])
            return (h / np.sqrt(size)).astype(np.float32)

        def _quantize_activations(x, bits=ACT_BITS):
            pos = 2 ** (bits - 1) - 1
            neg = 2 ** (bits - 1)
            scale = jnp.clip(jnp.max(jnp.abs(jax.lax.stop_gradient(x)), axis=-1, keepdims=True), 1e-05) / pos
            q = jnp.clip(jnp.round(x / scale), -neg, pos) * scale
            return x + jax.lax.stop_gradient(q - x)

        def _ternary_quantize_ste(w):
            scale = jnp.clip(jnp.mean(jnp.abs(jax.lax.stop_gradient(w)), axis=1, keepdims=True), 1e-05)
            n = w / scale
            tern = jnp.where(n > 0.5, 1.0, jnp.where(n < -0.5, -1.0, 0.0))
            q = tern * scale
            return w + jax.lax.stop_gradient(q - w)
        key = jax.random.key(seed)
        k1, k2 = jax.random.split(key)
        x = jax.random.normal(k1, (8, 4096, IN_FEATURES), dtype=jnp.float32)
        bound = 1.0 / np.sqrt(IN_FEATURES)
        weight = jax.random.uniform(k2, (512, IN_FEATURES), dtype=jnp.float32, minval=-bound, maxval=bound)
        return {'x': x, 'weight': weight}
    _L0_ffn_all = _L0_ffn_setup()
    _L0_ffn_in = {k: v for k, v in _L0_ffn_all.items() if k in ('weight',)}
    del _L0_ffn_all
    return {'x': x, 'ctx_1024': ctx_1024, 'L0_ffn_weight': _L0_ffn_in['weight']}

def reference(x, ctx_1024, L0_ffn_weight):
    import jax
    import jax.numpy as jnp

    def _L0_xattn_ref(Q, K):
        import jax, jax.numpy as jnp
        import numpy as np
        B, L, D = (4, 2048, 512)
        scores = jnp.einsum('btd,bsd->bts', K, K)
        Lq = Q.shape[1]
        mask = jnp.tril(jnp.ones((Lq, Lq), dtype=scores.dtype))
        scores = scores * mask[None, :, :]
        Q_proj = jnp.einsum('bts,bsd->btd', scores, Q)
        return Q + Q_proj

    def _L0_ffn_ref(x, weight):
        import jax, jax.numpy as jnp
        import numpy as np
        IN_FEATURES = 512
        ACT_BITS = 4

        def _hadamard(size: int) -> np.ndarray:
            h = np.array([[1.0]], dtype=np.float64)
            while h.shape[0] < size:
                h = np.block([[h, h], [h, -h]])
            return (h / np.sqrt(size)).astype(np.float32)

        def _quantize_activations(x, bits=ACT_BITS):
            pos = 2 ** (bits - 1) - 1
            neg = 2 ** (bits - 1)
            scale = jnp.clip(jnp.max(jnp.abs(jax.lax.stop_gradient(x)), axis=-1, keepdims=True), 1e-05) / pos
            q = jnp.clip(jnp.round(x / scale), -neg, pos) * scale
            return x + jax.lax.stop_gradient(q - x)

        def _ternary_quantize_ste(w):
            scale = jnp.clip(jnp.mean(jnp.abs(jax.lax.stop_gradient(w)), axis=1, keepdims=True), 1e-05)
            n = w / scale
            tern = jnp.where(n > 0.5, 1.0, jnp.where(n < -0.5, -1.0, 0.0))
            q = tern * scale
            return w + jax.lax.stop_gradient(q - w)
        H = jnp.asarray(_hadamard(IN_FEATURES))
        xh = x @ H
        xq = _quantize_activations(xh)
        wq = _ternary_quantize_ste(weight)
        return jnp.einsum('bsi,oi->bso', xq, wq)
    x = x + _L0_xattn_ref(_layernorm(x, axis=-1), ctx_1024)
    x = x + _L0_ffn_ref(_layernorm(x, axis=-1), L0_ffn_weight)
    return x

_drawn_inputs = setup_inputs


def setup_inputs(seed=0):
    import zlib

    import numpy as np

    out = dict(_drawn_inputs(seed))
    spreads = {}
    factors = {'L0_ffn_weight': 200.0}
    for name, (base, spread) in spreads.items():
        noise = np.random.default_rng([zlib.crc32(name.encode()), seed]).standard_normal(out[name].shape)
        drawn = base * np.exp(spread * noise) if base else spread * noise
        out[name] = jnp.asarray(drawn.astype(out[name].dtype))
    for name, factor in factors.items():
        out[name] = (out[name] * factor).astype(out[name].dtype)
    return out
```

```python
from contextlib import ExitStack

import concourse.bass as bass
from concourse import mybir

ALU = mybir.AluOpType
ACT = mybir.ActivationFunctionType
AX_X = mybir.AxisListType.X
F32 = mybir.dt.float32
F32R = mybir.dt.float32r
BF16 = mybir.dt.bfloat16

P = 128
B, L, D = 4, 1024, 512
NT = L // P
NC = D // P
HALF = L // 2
HT = NT // 2
EPS = 1e-5
QPOS, QNEG = 7.0, -8.0
QMIN = 1e-5
ROUND = 1.5 * 2.0**23

CONSTS = 3 * 16

ITEMS = [("kt", j) for j in range(NT)] + [("s0", j) for j in range(HT)] + [("s1", j) for j in range(NT)]
NI = len(ITEMS)
EARLY = NT + HT + 1
SLOTS = NT + 2
OWN = list(range(EARLY, NI))
FRONT_A = [[(0, OWN[2 * s])] for s in range(HT)] + [[(1, 2 * s)] for s in range(HT)] \
    + [[(1, NT)], [(1, NT + 2), (1, NT + 3)]]
FRONT_B = [[(0, k) for k in OWN[2 * s + 1:2 * s + 2]] for s in range(HT)] + [[(1, 2 * s + 1)] for s in range(HT)] \
    + [[(1, NT + 1)], [(1, NT + 4)]]


def score_span(kind, j):
    low, high = (0, HALF) if kind == "s0" else (HALF, L)
    return max(low, P * j), high


def score_base(kind, j):
    return sum(score_span(kind, i)[1] - score_span(kind, i)[0] for i in range(j))


def has_diagonal(kind, j):
    return kind != "kt" and score_span(kind, j)[0] == P * j


def diagonals_before(b, k):
    return NT * b + sum(has_diagonal(*ITEMS[i]) for i in range(k))


def build(nc, x_in, ctx_in, w_in, ident_in, had_in, mask_in, out):
    with ExitStack() as stack:
        def sb(name, shape, dt=F32):
            return stack.enter_context(nc.sbuf_tensor(name, shape, dt))

        def sem(name):
            return stack.enter_context(nc.semaphore(name))

        def bank(name):
            return stack.enter_context(nc.psum_tensor(name, [P, D], F32))

        ps_item = [bank(f"ps_item{i}") for i in range(2)]
        ps_att = [bank(f"ps_att{i}") for i in range(2)]
        ps_ut = bank("ps_ut")
        ps_had = bank("ps_had")
        ps_qt = bank("ps_qt")
        ps_ffn = bank("ps_ffn")

        ident = sb("ident", [P, P])
        ident_r = sb("ident_r", [P, P], F32R)
        had = sb("had", [P, P])
        had_r = sb("had_r", [P, P], F32R)
        mask = sb("mask", [P, P])
        mean_scales = sb("mean_scales", [P, 2])
        minus_half = sb("minus_half", [P, 1])
        round_up = sb("round_up", [P, 1])
        round_down = sb("round_down", [P, 1])
        eps = sb("eps", [P, 2])
        ones = sb("ones", [P, P])
        w_raw = sb("w_raw", [P, NC, D])
        w_abs = sb("w_abs", [P, NC])
        w_scale = sb("w_scale", [P, NC])
        w_thr = sb("w_thr", [P, NC])
        w_nthr = sb("w_nthr", [P, NC])
        w_tern = sb("w_tern", [P, NC, D])
        w_diag = sb("w_diag", [P, NC, P])
        w_t = sb("w_t", [P, NC, D], BF16)
        w_row = sb("w_row", [P, D])

        k_raw = sb("k_raw", [P, NT, D])
        kt_hi = sb("kt_hi", [P, NC, L], F32R)
        kt_lo = sb("kt_lo", [P, NC, L], F32R)
        x_raw = sb("x_raw", [P, NT, D])
        q_hi = sb("q_hi", [P, NT, D], F32R)
        q_lo = sb("q_lo", [P, NT, D], F32R)
        n_half = {"s0": score_base("s0", HT), "s1": score_base("s1", NT)}
        a_hi = {h: sb(f"a_hi_{h}", [P, n], F32R) for h, n in n_half.items()}
        a_lo = {h: sb(f"a_lo_{h}", [P, n], F32R) for h, n in n_half.items()}

        q_full = sb("q_full", [P, 2, D])
        z = sb("z", [P, 4, D])
        pairs = sb("pairs", [P, 2, NC, P])
        u = sb("u", [P, 2, NC, P])
        ut_hi = sb("ut_hi", [P, D], F32R)
        ut_lo = sb("ut_lo", [P, D], F32R)
        junk = sb("junk", [P, D])
        v = sb("v", [P, D])
        qt = sb("qt", [P, NC, P], BF16)
        y = sb("y", [P, 4, D])

        bn = sb("bn", [P, NT, 6])
        mv = sb("mv", [P, NT, 2])
        var_eps = sb("var_eps", [P, NT])
        rstd = sb("rstd", [P, NT])
        z_sum = sb("z_sum", [P, NT])
        z_mean = sb("z_mean", [P, NT, 2])
        z_sq = sb("z_sq", [P, NT])
        z_sq_eps = sb("z_sq_eps", [P, NT])
        z_rstd = sb("z_rstd", [P, NT])
        h_max = sb("h_max", [P, NT])
        h_top = sb("h_top", [P, NT])
        h_inv = sb("h_inv", [P, NT])
        q_inv = sb("q_inv", [P, NT])
        q_scale = sb("q_scale", [P, NT])

        const_in = sem("const_in")
        weight_in = sem("weight_in")
        k_in = [sem(f"k_in{j}") for j in range(NT)]
        x_in_sem = [sem(f"x_in{j}") for j in range(NT)]
        stored = [sem(f"stored{i}") for i in range(4)]
        item_done = sem("item_done")
        att_done = sem("att_done")
        ut_done = sem("ut_done")
        had_done = sem("had_done")
        qt_done = sem("qt_done")
        ffn_done = sem("ffn_done")
        wt_done = sem("wt_done")
        item_hi = sem("item_hi")
        q_hi_done = sem("q_hi_done")
        sq_done = sem("sq_done")
        ut_hi_done = sem("ut_hi_done")
        v_done = sem("v_done")
        qt_copied = sem("qt_copied")
        wt_copied = sem("wt_copied")
        dve_const = sem("dve_const")
        masked = sem("masked")
        item_lo = sem("item_lo")
        bn_done = sem("bn_done")
        mv_done = sem("mv_done")
        q_done = sem("q_done")
        z_done = sem("z_done")
        z_mean_done = sem("z_mean_done")
        u0_done = sem("u0_done")
        ut_lo_done = sem("ut_lo_done")
        max_done = sem("max_done")
        top_done = sem("top_done")
        inv_done = sem("inv_done")
        q_inv_done = sem("q_inv_done")
        clipped = sem("clipped")
        y_scaled = sem("y_scaled")
        w_step = sem("w_step")
        pool_const = sem("pool_const")
        var_eps_done = sem("var_eps_done")
        rstd_done = sem("rstd_done")
        q_lo_done = sem("q_lo_done")
        pairs_done = sem("pairs_done")
        u_done = sem("u_done")
        z_eps_done = sem("z_eps_done")
        z_rstd_done = sem("z_rstd_done")
        y_done = sem("y_done")

        k_rows = ctx_in.rearrange("b (j p) d -> p (b j) d", p=P)
        x_rows = x_in.rearrange("b (j p) d -> p (b j) d", p=P)
        out_rows = out.rearrange("b (j p) d -> p (b j) d", p=P)

        def f32(ap):
            return ap.bitcast(F32)

        def item_parts(k):
            kind, j = ITEMS[k]
            ps = ps_item[k % 2]
            if kind == "kt":
                rows = slice(P * j, P * j + P)
                return ps[:].rearrange("p (c t) -> p c t", c=NC), kt_hi[:, :, rows], kt_lo[:, :, rows]
            first, end = score_span(kind, j)
            at = score_base(kind, j)
            cols = slice(at, at + end - first)
            return ps[:, 0:end - first], a_hi[kind][:, cols], a_lo[kind][:, cols]

        block = stack.enter_context(nc.Block())

        @block.sync
        def _(sp):
            def load_k(b, j):
                sp.dma_start(k_raw[:, j:j + 1, :], k_rows[:, bass.ds(NT * b + j, 1), :]).then_inc(k_in[j], 16)

            def load_x(b, j):
                sp.dma_start(x_raw[:, j:j + 1, :], x_rows[:, bass.ds(NT * b + j, 1), :]).then_inc(x_in_sem[j], 16)

            def batch(b, last):
                for s in range(SLOTS):
                    if not last and s < HT:
                        for j in (2 * s, 2 * s + 1):
                            sp.wait_ge(item_done, NI * b + j + 1)
                            load_k(b + 1, j)
                    if not last and s < NT:
                        sp.wait_ge(z_done, NT * b + s + 1)
                        load_x(b + 1, s)
                    if s >= 2:
                        i = s - 2
                        sp.wait_ge(y_done, NT * b + i + 1)
                        sp.dma_start(out_rows[:, bass.ds(NT * b + i, 1), :], y[:, i % 4:i % 4 + 1, :]).then_inc(
                            stored[i % 4], 16)

            sp.dma_start(ident[:], ident_in).then_inc(const_in, 16)
            load_k(0, 0)
            load_k(0, 1)
            load_x(0, 0)
            sp.dma_start(had[:], had_in).then_inc(const_in, 16)
            sp.dma_start(mask[:], mask_in).then_inc(const_in, 16)
            for j in range(2, NT):
                load_k(0, j)
            sp.dma_start(w_raw[:], w_in.rearrange("(k p) i -> p k i", p=P)).then_inc(weight_in, 16)
            for j in range(1, NT):
                load_x(0, j)
            with sp.Fori(0, B - 1) as b:
                batch(b, False)
            batch(B - 1, True)
            for i in range(4):
                sp.wait_ge(stored[i], 16 * B * NT // 4)

        @block.tensor
        def _(pe):
            def item(b, k):
                kind, j = ITEMS[k]
                ps = ps_item[k % 2]
                if not (isinstance(b, int) and b == 0 and k < 2):
                    pe.wait_ge(item_lo, NI * b + k - 1)
                if kind == "kt":
                    pe.wait_ge(k_in[j], 16 * b + 16)
                    for c in range(NC):
                        last = nc.tensor.transpose(ps[:, P * c:P * c + P], k_raw[:, j, P * c:P * c + P], ident[:])
                    last.then_inc(item_done, 1)
                    return
                first, end = score_span(kind, j)
                pe.wait_ge(item_lo, NI * b + (HT if kind == "s0" else NT))
                n = end - first
                steps = [(c, l, r) for l, r in ((kt_hi, kt_hi), (kt_hi, kt_lo), (kt_lo, kt_hi)) for c in range(NC)]
                for n_step, (c, l, r) in enumerate(steps):
                    last = nc.tensor.matmul(ps[:, 0:n], l[:, c, P * j:P * j + P], r[:, c, first:end],
                                            start=(n_step == 0), stop=(n_step == len(steps) - 1 and first != P * j))
                if first == P * j:
                    last = nc.tensor.matmul(ps[:, 0:P], ident_r[:], ident_r[:], start=False, stop=True)
                last.then_inc(item_done, 1)

            def attention(b, i):
                kind = "s0" if i < HT else "s1"
                pe.wait_ge(item_lo, NI * b + ITEMS.index((kind, i)) + 1)
                pe.wait_ge(q_lo_done, NT * b + i + 1)
                pe.wait_ge(q_hi_done, NT * b + i + 1)
                n = 0
                for j in range(i + 1):
                    at = score_base(kind, j) + P * i - score_span(kind, j)[0]
                    for l, r in ((a_hi, q_hi), (a_hi, q_lo), (a_lo, q_hi)):
                        last = nc.tensor.matmul(ps_att[i % 2][:], l[kind][:, at:at + P], r[:, j, :],
                                                start=(n == 0), stop=(n == 3 * i + 2))
                        n += 1
                last.then_inc(att_done, 1)

            def transpose_u(b, i):
                pe.wait_ge(u_done, NT * b + i + 1)
                pe.wait_ge(u0_done, NT * b + i + 1)
                for c in range(NC):
                    last = nc.tensor.transpose(ps_ut[:, P * c:P * c + P], u[:, i % 2, c, :], ident[:])
                last.then_inc(ut_done, 1)

            def hadamard(b, i):
                pe.wait_ge(ut_lo_done, NT * b + i + 1)
                for c in range(NC):
                    cols = slice(P * c, P * c + P)
                    nc.tensor.matmul(ps_had[:, cols], ut_hi[:, cols], had_r[:], start=True, stop=False)
                    last = nc.tensor.matmul(ps_had[:, cols], ut_lo[:, cols], had_r[:], start=False, stop=True)
                last.then_inc(had_done, 1)

            def transpose_q(b, i):
                pe.wait_ge(clipped, NT * b + i + 1)
                for c in range(NC):
                    last = nc.tensor.transpose(ps_qt[:, P * c:P * c + P], v[:, P * c:P * c + P], ident[:])
                last.then_inc(qt_done, 1)

            def ffn(b, i):
                pe.wait_ge(qt_copied, NT * b + i + 1)
                pe.wait_ge(y_scaled, NT * b + i)
                for c in range(NC):
                    last = nc.tensor.matmul(ps_ffn[:], qt[:, c, :], w_t[:, c, :], start=(c == 0), stop=(c == NC - 1))
                last.then_inc(ffn_done, 1)

            def batch(b, last):
                for s in range(SLOTS):
                    for off, k in FRONT_A[s]:
                        if not (last and off):
                            item(b + off, k)
                    if s < NT:
                        attention(b, s)
                    if 1 <= s <= NT:
                        transpose_u(b, s - 1)
                    if s >= 2:
                        transpose_q(b, s - 2)
                    for off, k in FRONT_B[s]:
                        if not (last and off):
                            item(b + off, k)
                    if s >= 2:
                        ffn(b, s - 2)
                    if 1 <= s <= NT:
                        hadamard(b, s - 1)

            pe.wait_ge(const_in, CONSTS)
            for k in range(NT):
                item(0, k)
            pe.wait_ge(dve_const, 2)
            for k in range(NT, EARLY):
                item(0, k)
            for c in range(NC):
                pe.wait_ge(w_step, 3 * NC + 4)
                if c >= 2:
                    pe.wait_ge(wt_copied, c - 1)
                for k in range(NC):
                    last = nc.tensor.transpose(ps_att[c % 2][:, P * k:P * k + P], w_tern[:, k, P * c:P * c + P], ident[:])
                last.then_inc(wt_done, 1)
            for k in range(NC):
                last = nc.tensor.matmul(ps_ffn[:, P * k:P * k + P], ones[:], w_diag[:, k, :], start=True, stop=True)
            last.then_inc(wt_done, 1)
            pe.wait_ge(wt_copied, NC)
            with pe.Fori(0, B - 1) as b:
                batch(b, False)
            batch(B - 1, True)

        @block.scalar
        def _(act):
            def item(b, k):
                ps, hi, _ = item_parts(k)
                if has_diagonal(*ITEMS[k]):
                    act.wait_ge(masked, diagonals_before(b, k) + 1)
                else:
                    act.wait_ge(item_done, NI * b + k + 1)
                nc.scalar.copy(hi, ps).then_inc(item_hi, 1)

            def values_hi(b, i):
                act.wait_ge(q_done, NT * b + i + 1)
                nc.scalar.copy(q_hi[:, i, :], q_full[:, i % 2, :]).then_inc(q_hi_done, 1)

            def square(b, i):
                act.wait_ge(z_mean_done, NT * b + i + 1)
                nc.scalar.activation(junk[:], z[:, i % 4, :], ACT.Square, bias=z_mean[:, i, 0:1],
                                     accum_out=z_sq[:, i:i + 1]).then_inc(sq_done, 1)

            def split_u(b, i):
                act.wait_ge(ut_done, NT * b + i + 1)
                nc.scalar.copy(ut_hi[:], ps_ut[:]).then_inc(ut_hi_done, 1)

            def quantise(b, i):
                act.wait_ge(q_inv_done, NT * b + i + 1)
                nc.scalar.activation(v[:], ps_had[:], ACT.Identity, bias=round_up[:],
                                     scale=q_inv[:, i:i + 1]).then_inc(v_done, 1)

            def copy_qt(b, i):
                act.wait_ge(qt_done, NT * b + i + 1)
                nc.scalar.activation(qt[:], ps_qt[:].rearrange("p (c t) -> p c t", c=NC), ACT.Identity,
                                     bias=round_down[:]).then_inc(qt_copied, 1)

            def batch(b, last):
                for s in range(SLOTS):
                    for off, k in FRONT_A[s]:
                        if not (last and off):
                            item(b + off, k)
                    if s >= 2:
                        quantise(b, s - 2)
                    if 1 <= s <= NT:
                        split_u(b, s - 1)
                    if s < NT:
                        square(b, s)
                    if s >= 2:
                        copy_qt(b, s - 2)
                    for off, k in FRONT_B[s]:
                        if not (last and off):
                            item(b + off, k)
                    if s < NT - 1:
                        values_hi(b, s + 1)
                    if s == NT and not last:
                        values_hi(b + 1, 0)

            for k in range(NT):
                item(0, k)
            values_hi(0, 0)
            for k in range(NT, EARLY):
                item(0, k)
            for c in range(NC):
                act.wait_ge(wt_done, c + 1)
                nc.scalar.copy(w_t[:, c, :], ps_att[c % 2][:]).then_inc(wt_copied, 1)
            act.wait_ge(pool_const, 5)
            with act.Fori(0, B - 1) as b:
                batch(b, False)
            batch(B - 1, True)

        @block.vector
        def _(dve):
            def item(b, k):
                ps, hi, lo = item_parts(k)
                if has_diagonal(*ITEMS[k]):
                    dve.wait_ge(item_done, NI * b + k + 1)
                    nc.vector.tensor_tensor(ps[:, 0:P], ps[:, 0:P], mask[:], ALU.mult).then_inc(masked, 1)
                dve.wait_ge(item_hi, NI * b + k + 1)
                nc.vector.tensor_tensor(lo, ps, f32(hi), ALU.subtract).then_inc(item_lo, 1)

            def statistics(b, i):
                dve.wait_ge(x_in_sem[i], 16 * b + 16)
                nc.vector.bn_stats(bn[:, i, :], x_raw[:, i, :])

            def mean_variance(i):
                nc.vector.bn_aggr(mv[:, i, :], bn[:, i, :]).then_inc(mv_done, 1)

            def values(b, i):
                dve.wait_ge(rstd_done, NT * b + i + 1)
                nc.vector.tensor_scalar(q_full[:, i % 2, :], x_raw[:, i, :], mv[:, i, 0:1], rstd[:, i:i + 1],
                                        ALU.subtract, ALU.mult).then_inc(q_done, 1)

            def residual(b, i):
                dve.wait_ge(att_done, NT * b + i + 1)
                nc.vector.scalar_tensor_tensor(out=z[:, i % 4, :], in0=ps_att[i % 2][:], scalar=1.0, in1=x_raw[:, i, :],
                                               op0=ALU.mult, op1=ALU.add,
                                               accum_out=z_sum[:, i:i + 1]).then_inc(z_done, 1)
                dve.wait_ge(z_done, NT * b + i + 1)
                nc.vector.tensor_scalar(z_mean[:, i, :], mean_scales[:], z_sum[:, i:i + 1], None,
                                        ALU.mult).then_inc(z_mean_done, 1)

            def first_chunk(b, i):
                dve.wait_ge(pairs_done, 2 * (NT * b + i) + 1)
                dve.wait_ge(z_mean_done, NT * b + i + 1)
                nc.vector.scalar_tensor_tensor(out=u[:, i % 2, 0, :], in0=pairs[:, i % 2, 0, :],
                                               scalar=z_mean[:, i, 1:2], in1=pairs[:, i % 2, 1, :],
                                               op0=ALU.subtract, op1=ALU.add).then_inc(u0_done, 1)

            def split_u(b, i):
                dve.wait_ge(ut_hi_done, NT * b + i + 1)
                nc.vector.tensor_tensor(ut_lo[:], ps_ut[:], f32(ut_hi[:]), ALU.subtract).then_inc(ut_lo_done, 1)

            def row_scale(b, i):
                at = slice(i, i + 1)
                dve.wait_ge(had_done, NT * b + i + 1)
                nc.vector.tensor_reduce(h_max[:, at], ps_had[:], AX_X, ALU.max,
                                        apply_absolute_value=True).then_inc(max_done, 1)
                dve.wait_ge(max_done, NT * b + i + 1)
                dve.wait_ge(z_rstd_done, NT * b + i + 1)
                nc.vector.tensor_scalar(h_top[:, at], h_max[:, at], z_rstd[:, at], QMIN, ALU.mult,
                                        ALU.max).then_inc(top_done, 1)
                dve.wait_ge(top_done, NT * b + i + 1)
                nc.vector.reciprocal(h_inv[:, at], h_top[:, at]).then_inc(inv_done, 1)
                nc.vector.tensor_scalar(q_scale[:, at], h_top[:, at], 1.0 / QPOS, None, ALU.mult)
                dve.wait_ge(inv_done, NT * b + i + 1)
                nc.vector.tensor_scalar(q_inv[:, at], h_inv[:, at], z_rstd[:, at], QPOS, ALU.mult,
                                        ALU.mult).then_inc(q_inv_done, 1)

            def clip(b, i):
                dve.wait_ge(v_done, NT * b + i + 1)
                nc.vector.tensor_scalar(v[:], v[:], ROUND + QNEG, ROUND + QPOS, ALU.max, ALU.min).then_inc(clipped, 1)

            def scale_ffn(b, i):
                dve.wait_ge(ffn_done, NT * b + i + 1)
                dve.wait_ge(stored[i % 4], 16 * (2 * b + i // 4))
                nc.vector.scalar_tensor_tensor(out=y[:, i % 4, :], in0=ps_ffn[:], scalar=q_scale[:, i:i + 1],
                                               in1=w_row[:], op0=ALU.mult, op1=ALU.mult).then_inc(y_scaled, 1)

            def batch(b, last):
                for s in range(SLOTS):
                    for off, k in FRONT_A[s]:
                        if not (last and off):
                            item(b + off, k)
                    if s >= 2:
                        clip(b, s - 2)
                    if s < NT - 1:
                        statistics(b, s + 1)
                    if s == NT - 1 and not last:
                        statistics(b + 1, 0)
                    if s < NT:
                        residual(b, s)
                    if s < NT - 1 or (s == NT - 1 and not last):
                        mean_variance((s + 1) % NT)
                    if 1 <= s <= NT:
                        split_u(b, s - 1)
                    if s < NT:
                        first_chunk(b, s)
                    if s < NT - 1:
                        values(b, s + 1)
                    if s == NT and not last:
                        values(b + 1, 0)
                    for off, k in FRONT_B[s]:
                        if not (last and off):
                            item(b + off, k)
                    if s >= 2:
                        scale_ffn(b, s - 2)
                    if 1 <= s <= NT:
                        row_scale(b, s - 1)

            nc.vector.memset(mean_scales[:, 0:1], -1.0 / D)
            nc.vector.memset(mean_scales[:, 1:2], NC / D)
            nc.vector.memset(ones[:], 1.0)
            dve.wait_ge(const_in, CONSTS)
            nc.vector.tensor_copy(ident_r[:], ident[:]).then_inc(dve_const, 1)
            nc.vector.tensor_copy(had_r[:], had[:]).then_inc(dve_const, 1)
            for k in range(HT):
                item(0, k)
            dve.wait_ge(x_in_sem[0], 16)
            nc.vector.bn_stats(bn[:, 0, :], x_raw[:, 0, :]).then_inc(bn_done, 1)
            dve.wait_ge(bn_done, 1)
            mean_variance(0)
            for k in range(HT, NT):
                item(0, k)
            values(0, 0)
            for k in range(NT, EARLY):
                item(0, k)
            dve.wait_ge(weight_in, 16)
            nc.vector.tensor_reduce(w_abs[:], w_raw[:], AX_X, ALU.add, apply_absolute_value=True).then_inc(w_step, 1)
            dve.wait_ge(w_step, 1)
            nc.vector.tensor_scalar(w_scale[:], w_abs[:], 1.0 / D, QMIN, ALU.mult, ALU.max).then_inc(w_step, 1)
            dve.wait_ge(w_step, 2)
            for k in range(NC):
                nc.vector.tensor_scalar(w_diag[:, k, :], ident[:], w_scale[:, k:k + 1], None, ALU.mult).then_inc(w_step, 1)
            nc.vector.tensor_scalar(w_thr[:], w_scale[:], 0.5, None, ALU.mult).then_inc(w_step, 1)
            nc.vector.tensor_scalar(w_nthr[:], w_scale[:], -0.5, None, ALU.mult).then_inc(w_step, 1)
            dve.wait_ge(w_step, NC + 4)
            for k in range(NC):
                nc.vector.tensor_scalar(w_tern[:, k, :], w_raw[:, k, :], w_nthr[:, k:k + 1], None,
                                        ALU.is_lt).then_inc(w_step, 1)
            for k in range(NC):
                dve.wait_ge(w_step, NC + 5 + k)
                nc.vector.scalar_tensor_tensor(out=w_tern[:, k, :], in0=w_raw[:, k, :], scalar=w_thr[:, k:k + 1],
                                               in1=w_tern[:, k, :], op0=ALU.is_gt, op1=ALU.subtract).then_inc(w_step, 1)
            dve.wait_ge(wt_done, NC + 1)
            nc.vector.tensor_copy(w_row[:], ps_ffn[:]).then_inc(w_step, 1)
            with dve.Fori(0, B - 1) as b:
                batch(b, False)
            batch(B - 1, True)

        @block.gpsimd
        def _(pool):
            def norm(b, i):
                at = slice(i, i + 1)
                pool.wait_ge(mv_done, NT * b + i + 1)
                nc.gpsimd.tensor_tensor(var_eps[:, at], mv[:, i, 1:2], eps[:, 0:1], ALU.add).then_inc(var_eps_done, 1)
                pool.wait_ge(var_eps_done, NT * b + i + 1)
                nc.gpsimd.tensor_tensor(rstd[:, at], var_eps[:, at], minus_half[:], ALU.pow).then_inc(rstd_done, 1)

            def values_lo(b, i):
                pool.wait_ge(q_hi_done, NT * b + i + 1)
                nc.gpsimd.tensor_tensor(q_lo[:, i, :], q_full[:, i % 2, :], f32(q_hi[:, i, :]),
                                        ALU.subtract).then_inc(q_lo_done, 1)

            def butterflies(b, i):
                r = i % 2
                pool.wait_ge(z_done, NT * b + i + 1)
                lower, upper = z[:, i % 4, 0:2 * P], z[:, i % 4, 2 * P:4 * P]
                p = pairs[:, r, :, :].rearrange("p c t -> p (c t)")
                nc.gpsimd.tensor_tensor(p[:, 0:2 * P], lower, upper, ALU.add).then_inc(pairs_done, 1)
                nc.gpsimd.tensor_tensor(p[:, 2 * P:4 * P], lower, upper, ALU.subtract).then_inc(pairs_done, 1)
                pool.wait_ge(pairs_done, 2 * (NT * b + i) + 2)
                nc.gpsimd.tensor_tensor(u[:, r, 2, :], pairs[:, r, 2, :], pairs[:, r, 3, :], ALU.add)
                both = pairs[:, r, :, :].rearrange("p (g h) t -> p g h t", h=2)
                to = u[:, r, :, :].rearrange("p (g h) t -> p g h t", h=2)
                nc.gpsimd.tensor_tensor(to[:, :, 1, :], both[:, :, 0, :], both[:, :, 1, :], ALU.subtract).then_inc(u_done, 1)

            def norm_z(b, i):
                at = slice(i, i + 1)
                pool.wait_ge(sq_done, NT * b + i + 1)
                nc.gpsimd.tensor_tensor(z_sq_eps[:, at], z_sq[:, at], eps[:, 1:2], ALU.add).then_inc(z_eps_done, 1)
                pool.wait_ge(z_eps_done, NT * b + i + 1)
                nc.gpsimd.tensor_tensor(z_rstd[:, at], z_sq_eps[:, at], minus_half[:], ALU.pow).then_inc(z_rstd_done, 1)

            def add_z(b, i):
                pool.wait_ge(y_scaled, NT * b + i + 1)
                nc.gpsimd.tensor_tensor(y[:, i % 4, :], y[:, i % 4, :], z[:, i % 4, :], ALU.add).then_inc(y_done, 1)

            def batch(b, last):
                for s in range(SLOTS):
                    if s < NT - 1:
                        norm(b, s + 1)
                    if s == NT and not last:
                        norm(b + 1, 0)
                    if s < NT:
                        butterflies(b, s)
                        norm_z(b, s)
                    if s < NT - 1:
                        values_lo(b, s + 1)
                    if s == NT and not last:
                        values_lo(b + 1, 0)
                    if s >= 2:
                        add_z(b, s - 2)

            nc.gpsimd.memset(minus_half[:], -0.5).then_inc(pool_const, 1)
            nc.gpsimd.memset(round_up[:], ROUND).then_inc(pool_const, 1)
            nc.gpsimd.memset(round_down[:], -ROUND).then_inc(pool_const, 1)
            nc.gpsimd.memset(eps[:, 0:1], EPS).then_inc(pool_const, 1)
            nc.gpsimd.memset(eps[:, 1:2], D * EPS).then_inc(pool_const, 1)
            pool.wait_ge(pool_const, 5)
            norm(0, 0)
            values_lo(0, 0)
            with pool.Fori(0, B - 1) as b:
                batch(b, False)
            batch(B - 1, True)


def kernel(x, ctx_1024, L0_ffn_weight):
    import numpy as np
    import concourse.bacc as bacc
    from concourse import mybir as mb
    from concourse.bass_utils import run_bass_kernel_spmd

    had = np.ones((1, 1), np.float32)
    while had.shape[0] < P:
        had = np.block([[had, had], [had, -had]])
    arrays = {
        "x_dram": np.ascontiguousarray(x),
        "ctx_dram": np.ascontiguousarray(ctx_1024),
        "weight_dram": np.ascontiguousarray(L0_ffn_weight),
        "ident_dram": np.eye(P, dtype=np.float32),
        "had_dram": np.ascontiguousarray(had, dtype=np.float32),
        "mask_dram": np.triu(np.ones((P, P), np.float32)),
    }
    nc = bacc.Bacc("TRN2", target_bir_lowering=False, num_devices=1)
    args = [nc.dram_tensor(n, a.shape, mb.dt.from_np(a.dtype), kind="ExternalInput").ap() for n, a in arrays.items()]
    out = nc.dram_tensor("out_dram", (B, L, D), mb.dt.float32, kind="ExternalOutput").ap()
    build(nc, *args, out)
    r = run_bass_kernel_spmd(nc, [arrays], core_ids=[0])
    return r.results[0]["out_dram"]
```

```python
from contextlib import ExitStack

import concourse.bass as bass
from concourse import mybir

ALU = mybir.AluOpType
ACT = mybir.ActivationFunctionType
AX_X = mybir.AxisListType.X
F32 = mybir.dt.float32
F32R = mybir.dt.float32r
BF16 = mybir.dt.bfloat16

P = 128
B, L, D = 4, 1024, 512
NT = L // P
NC = D // P
HALF = L // 2
HT = NT // 2
EPS = 1e-5
QPOS, QNEG = 7.0, -8.0
QMIN = 1e-5
ROUND = 1.5 * 2.0**23

CONSTS = 2 * 16

ITEMS = [("kt", j) for j in range(NT)] + [("s0", j) for j in range(HT)] + [("s1", j) for j in (0, 1, 2, 3, 5, 4, 6, 7)]
NI = len(ITEMS)
SLOTS = NT + 2
FRONT_A = [[(0, 14)], [(0, 15)], [(0, 17)], [(0, 18), (0, 19)], [(1, 0)], [(1, 2)], [(1, 4)], [(1, 6)],
           [(1, 8)], [(1, 10), (1, 11), (1, 12)]]
FRONT_B = [[], [(0, 16)], [], [], [(1, 1)], [(1, 3)], [(1, 5)], [(1, 7)],
           [(1, 9)], [(1, 13)]]
EARLY = 14
AHEAD = 2


def score_span(kind, j):
    low, high = (0, HALF) if kind == "s0" else (HALF, L)
    return max(low, P * j), high


def score_base(kind, j):
    return sum(score_span(kind, i)[1] - score_span(kind, i)[0] for i in range(j))


def has_diagonal(kind, j):
    return kind != "kt" and score_span(kind, j)[0] == P * j


def diagonals_before(b, k):
    return NT * b + sum(has_diagonal(*ITEMS[i]) for i in range(k))


def build(nc, x_in, ctx_in, w_in, ident_in, had_in, mask_in, out):
    with ExitStack() as stack:
        def sb(name, shape, dt=F32):
            return stack.enter_context(nc.sbuf_tensor(name, shape, dt))

        def sem(name):
            return stack.enter_context(nc.semaphore(name))

        def bank(name):
            return stack.enter_context(nc.psum_tensor(name, [P, D], F32))

        ps_item = [bank(f"ps_item{i}") for i in range(2)]
        ps_att = [bank(f"ps_att{i}") for i in range(2)]
        ps_ut = bank("ps_ut")
        ps_had = bank("ps_had")
        ps_qt = bank("ps_qt")
        ps_ffn = bank("ps_ffn")

        ident = sb("ident", [P, P])
        ident_r = sb("ident_r", [P, P], F32R)
        had = sb("had", [P, P])
        had_r = sb("had_r", [P, P], F32R)
        mask = sb("mask", [P, P])
        mean_scales = sb("mean_scales", [P, 2])
        minus_half = sb("minus_half", [P, 1])
        round_up = sb("round_up", [P, 1])
        round_down = sb("round_down", [P, 1])
        eps = sb("eps", [P, 2])
        ones = sb("ones", [P, P])
        w_raw = sb("w_raw", [P, NC, D])
        w_abs = sb("w_abs", [P, NC])
        w_scale = sb("w_scale", [P, NC])
        w_thr = sb("w_thr", [P, NC])
        w_nthr = sb("w_nthr", [P, NC])
        w_above = sb("w_above", [P, NC, D], BF16)
        w_below = sb("w_below", [P, NC, D], BF16)
        w_tern = sb("w_tern", [P, NC, D])
        w_diag = sb("w_diag", [P, NC, P])
        w_t = sb("w_t", [P, NC, D], BF16)
        w_row = sb("w_row", [P, D])

        k_raw = sb("k_raw", [P, NT, D])
        kt_hi = sb("kt_hi", [P, NC, L], F32R)
        kt_lo = sb("kt_lo", [P, NC, L], F32R)
        x_raw = sb("x_raw", [P, NT, D])
        q_hi = sb("q_hi", [P, NT, D], F32R)
        q_lo = sb("q_lo", [P, NT, D], F32R)
        n_half = {"s0": score_base("s0", HT), "s1": score_base("s1", NT)}
        a_hi = {h: sb(f"a_hi_{h}", [P, n], F32R) for h, n in n_half.items()}
        a_lo = {h: sb(f"a_lo_{h}", [P, n], F32R) for h, n in n_half.items()}

        q_full = sb("q_full", [P, 2, D])
        z = sb("z", [P, 4, D])
        pairs = sb("pairs", [P, 2, NC, P])
        u = sb("u", [P, 2, NC, P])
        ut_hi = sb("ut_hi", [P, D], F32R)
        ut_lo = sb("ut_lo", [P, D], F32R)
        junk = sb("junk", [P, D])
        v = sb("v", [P, D])
        qt = sb("qt", [P, NC, P], BF16)
        y = sb("y", [P, 4, D])

        bn = sb("bn", [P, NT, 6])
        mv = sb("mv", [P, NT, 2])
        var_eps = sb("var_eps", [P, NT])
        rstd = sb("rstd", [P, NT])
        z_sum = sb("z_sum", [P, NT])
        z_mean = sb("z_mean", [P, NT, 2])
        z_sq = sb("z_sq", [P, NT])
        z_sq_eps = sb("z_sq_eps", [P, NT])
        z_rstd = sb("z_rstd", [P, NT])
        h_max = sb("h_max", [P, NT])
        h_top = sb("h_top", [P, NT])
        h_inv = sb("h_inv", [P, NT])
        q_inv = sb("q_inv", [P, NT])
        q_scale = sb("q_scale", [P, NT])

        const_in = sem("const_in")
        ident_in_sem = sem("ident_in_sem")
        weight_in = sem("weight_in")
        k_in = [sem(f"k_in{j}") for j in range(NT)]
        x_in_sem = [sem(f"x_in{j}") for j in range(NT)]
        stored = [sem(f"stored{i}") for i in range(4)]
        item_done = sem("item_done")
        att_done = sem("att_done")
        ut_done = sem("ut_done")
        had_done = sem("had_done")
        qt_done = sem("qt_done")
        ffn_done = sem("ffn_done")
        wt_done = sem("wt_done")
        item_hi = sem("item_hi")
        q_hi_done = sem("q_hi_done")
        sq_done = sem("sq_done")
        ut_hi_done = sem("ut_hi_done")
        v_done = sem("v_done")
        qt_copied = sem("qt_copied")
        wt_copied = sem("wt_copied")
        dve_const = sem("dve_const")
        masked = sem("masked")
        item_lo = sem("item_lo")
        bn_done = sem("bn_done")
        mv_done = sem("mv_done")
        q_done = sem("q_done")
        z_done = sem("z_done")
        z_mean_done = sem("z_mean_done")
        u0_done = sem("u0_done")
        ut_lo_done = sem("ut_lo_done")
        max_done = sem("max_done")
        top_done = sem("top_done")
        inv_done = sem("inv_done")
        q_inv_done = sem("q_inv_done")
        clipped = sem("clipped")
        y_scaled = sem("y_scaled")
        w_step = sem("w_step")
        w_row_sum = sem("w_row_sum")
        w_row_done = sem("w_row_done")
        w_abs_done = sem("w_abs_done")
        w_cmp = sem("w_cmp")
        w_tern_done = sem("w_tern_done")
        pool_const = sem("pool_const")
        var_eps_done = sem("var_eps_done")
        rstd_done = sem("rstd_done")
        q_lo_done = sem("q_lo_done")
        pairs_done = sem("pairs_done")
        u_done = sem("u_done")
        z_eps_done = sem("z_eps_done")
        z_rstd_done = sem("z_rstd_done")
        y_done = sem("y_done")

        k_rows = ctx_in.rearrange("b (j p) d -> p (b j) d", p=P)
        x_rows = x_in.rearrange("b (j p) d -> p (b j) d", p=P)
        out_rows = out.rearrange("b (j p) d -> p (b j) d", p=P)

        def f32(ap):
            return ap.bitcast(F32)

        first_banks = ps_item + ps_att + [ps_ut, ps_had, ps_qt, ps_ffn]

        def is_first(b, k):
            return isinstance(b, int) and b == 0 and k < NT

        def item_parts(b, k):
            kind, j = ITEMS[k]
            ps = first_banks[k] if is_first(b, k) else ps_item[k % 2]
            if kind == "kt":
                rows = slice(P * j, P * j + P)
                return ps[:].rearrange("p (c t) -> p c t", c=NC), kt_hi[:, :, rows], kt_lo[:, :, rows]
            first, end = score_span(kind, j)
            at = score_base(kind, j)
            cols = slice(at, at + end - first)
            return ps[:, 0:end - first], a_hi[kind][:, cols], a_lo[kind][:, cols]

        block = stack.enter_context(nc.Block())

        @block.sync
        def _(sp):
            def load_k(b, j):
                sp.dma_start(k_raw[:, j:j + 1, :], k_rows[:, bass.ds(NT * b + j, 1), :]).then_inc(k_in[j], 16)

            def load_x(b, j):
                sp.dma_start(x_raw[:, j:j + 1, :], x_rows[:, bass.ds(NT * b + j, 1), :]).then_inc(x_in_sem[j], 16)

            def batch(b, last):
                for s in range(SLOTS):
                    if not last and s < HT:
                        for j in (2 * s, 2 * s + 1):
                            sp.wait_ge(item_done, NI * b + j + 1)
                            load_k(b + 1, j)
                    if not last and s < NT:
                        sp.wait_ge(z_done, NT * b + s + 1)
                        load_x(b + 1, s)
                    if s >= 3:
                        i = s - 3
                        sp.wait_ge(y_done, NT * b + i + 1)
                        sp.dma_start(out_rows[:, bass.ds(NT * b + i, 1), :], y[:, i % 4:i % 4 + 1, :]).then_inc(
                            stored[i % 4], 16)
                i = NT - 1
                sp.wait_ge(y_done, NT * b + i + 1)
                sp.dma_start(out_rows[:, bass.ds(NT * b + i, 1), :], y[:, i % 4:i % 4 + 1, :]).then_inc(
                    stored[i % 4], 16)

            load_k(0, 0)
            sp.dma_start(ident[:], ident_in).then_inc(ident_in_sem, 16)
            for j in range(1, HT):
                load_k(0, j)
            load_x(0, 0)
            for j in range(HT, NT):
                load_k(0, j)
            sp.dma_start(had[:], had_in).then_inc(const_in, 16)
            sp.dma_start(mask[:], mask_in).then_inc(const_in, 16)
            load_x(0, 1)
            sp.dma_start(w_raw[:], w_in.rearrange("(k p) i -> p k i", p=P)).then_inc(weight_in, 16)
            for j in range(2, NT):
                load_x(0, j)
            with sp.Fori(0, B - 1) as b:
                batch(b, False)
            batch(B - 1, True)
            for i in range(4):
                sp.wait_ge(stored[i], 16 * B * NT // 4)

        @block.tensor
        def _(pe):
            def item(b, k):
                kind, j = ITEMS[k]
                ps = first_banks[k] if is_first(b, k) else ps_item[k % 2]
                if not is_first(b, k):
                    pe.wait_ge(item_lo, NI * b + k - 1)
                if kind == "kt":
                    pe.wait_ge(k_in[j], 16 * b + 16)
                    for c in range(NC):
                        last = nc.tensor.transpose(ps[:, P * c:P * c + P], k_raw[:, j, P * c:P * c + P], ident[:])
                    last.then_inc(item_done, 1)
                    return
                first, end = score_span(kind, j)
                pe.wait_ge(item_lo, NI * b + (HT if kind == "s0" else NT))
                n = end - first
                steps = [(c, l, r) for l, r in ((kt_hi, kt_hi), (kt_hi, kt_lo), (kt_lo, kt_hi)) for c in range(NC)]
                for n_step, (c, l, r) in enumerate(steps):
                    last = nc.tensor.matmul(ps[:, 0:n], l[:, c, P * j:P * j + P], r[:, c, first:end],
                                            start=(n_step == 0), stop=(n_step == len(steps) - 1 and first != P * j))
                if first == P * j:
                    last = nc.tensor.matmul(ps[:, 0:P], ident_r[:], ident_r[:], start=False, stop=True)
                last.then_inc(item_done, 1)

            def attention(b, i, steps):
                kind = "s0" if i < HT else "s1"
                if steps[0] == 0:
                    pe.wait_ge(item_lo, NI * b + max(ITEMS.index((kind, j)) for j in range(i + 1)) + 1)
                    pe.wait_ge(q_lo_done, NT * b + i + 1)
                    pe.wait_ge(q_hi_done, NT * b + i + 1)
                for n in range(*steps):
                    j = n // 3
                    at = score_base(kind, j) + P * i - score_span(kind, j)[0]
                    l, r = ((a_hi, q_hi), (a_hi, q_lo), (a_lo, q_hi))[n % 3]
                    last = nc.tensor.matmul(ps_att[i % 2][:], l[kind][:, at:at + P], r[:, j, :],
                                            start=(n == 0), stop=(n == 3 * i + 2))
                if n == 3 * i + 2:
                    last.then_inc(att_done, 1)

            def transpose_u(b, i):
                pe.wait_ge(u_done, NT * b + i + 1)
                pe.wait_ge(u0_done, NT * b + i + 1)
                for c in range(NC):
                    last = nc.tensor.transpose(ps_ut[:, P * c:P * c + P], u[:, i % 2, c, :], ident[:])
                last.then_inc(ut_done, 1)

            def hadamard(b, i):
                pe.wait_ge(ut_lo_done, NT * b + i + 1)
                for c in range(NC):
                    cols = slice(P * c, P * c + P)
                    nc.tensor.matmul(ps_had[:, cols], ut_hi[:, cols], had_r[:], start=True, stop=False)
                    last = nc.tensor.matmul(ps_had[:, cols], ut_lo[:, cols], had_r[:], start=False, stop=True)
                last.then_inc(had_done, 1)

            def transpose_q(b, i):
                pe.wait_ge(clipped, NT * b + i + 1)
                for c in range(NC):
                    last = nc.tensor.transpose(ps_qt[:, P * c:P * c + P], v[:, P * c:P * c + P], ident[:])
                last.then_inc(qt_done, 1)

            def ffn(b, i):
                pe.wait_ge(qt_copied, NT * b + i + 1)
                pe.wait_ge(y_scaled, NT * b + i)
                for c in range(NC):
                    last = nc.tensor.matmul(ps_ffn[:], qt[:, c, :], w_t[:, c, :], start=(c == 0), stop=(c == NC - 1))
                last.then_inc(ffn_done, 1)

            def front(b, items, last):
                for off, k in items:
                    if not (last and off):
                        item(b + off, k)

            def batch(b, last):
                for s in range(SLOTS):
                    total = 3 * (s + 1)
                    first = total - 7 if HT <= s < NT else total if s == 0 else 0
                    if s == 0:
                        attention(b, s, (0, first))
                    front(b, FRONT_A[s], last)
                    if s and first:
                        attention(b, s, (0, first))
                    if 1 <= s <= NT:
                        transpose_u(b, s - 1)
                    if s >= 2:
                        transpose_q(b, s - 2)
                    front(b, FRONT_B[s], last)
                    if 0 < s < NT:
                        attention(b, s, (first, total))
                    if s >= 2:
                        ffn(b, s - 2)
                    if 1 <= s <= NT:
                        hadamard(b, s - 1)

            pe.wait_ge(ident_in_sem, 16)
            for k in range(NT):
                item(0, k)
            pe.wait_ge(dve_const, 2)
            for k in range(NT, NT + HT):
                item(0, k)
            for c in range(NC):
                if c == 0:
                    pe.wait_ge(w_tern_done, NC)
                else:
                    pe.wait_ge(wt_copied, c)
                for k in range(NC):
                    last = nc.tensor.transpose(ps_att[1][:, P * k:P * k + P], w_tern[:, k, P * c:P * c + P], ident[:])
                last.then_inc(wt_done, 1)
                if c == 0:
                    pe.wait_ge(w_step, NC + 3)
                    for k in range(NC):
                        last = nc.tensor.matmul(ps_ffn[:, P * k:P * k + P], ones[:], w_diag[:, k, :], start=True, stop=True)
                    last.then_inc(w_row_sum, 1)
                if c in (1, 2):
                    item(0, NT + HT + c - 1)
            pe.wait_ge(wt_copied, NC)
            with pe.Fori(0, B - 1) as b:
                batch(b, False)
            batch(B - 1, True)

        @block.scalar
        def _(act):
            def item(b, k):
                ps, hi, _ = item_parts(b, k)
                if has_diagonal(*ITEMS[k]):
                    act.wait_ge(masked, diagonals_before(b, k) + 1)
                else:
                    act.wait_ge(item_done, NI * b + k + 1)
                nc.scalar.copy(hi, ps).then_inc(item_hi, 1)

            def values_hi(b, i):
                act.wait_ge(q_done, NT * b + i + 1)
                nc.scalar.copy(q_hi[:, i, :], q_full[:, i % 2, :]).then_inc(q_hi_done, 1)

            def square(b, i):
                act.wait_ge(z_mean_done, NT * b + i + 1)
                nc.scalar.activation(junk[:], z[:, i % 4, :], ACT.Square, bias=z_mean[:, i, 0:1],
                                     accum_out=z_sq[:, i:i + 1]).then_inc(sq_done, 1)

            def split_u(b, i):
                act.wait_ge(ut_done, NT * b + i + 1)
                nc.scalar.copy(ut_hi[:], ps_ut[:]).then_inc(ut_hi_done, 1)

            def quantise(b, i):
                act.wait_ge(q_inv_done, NT * b + i + 1)
                nc.scalar.activation(v[:], ps_had[:], ACT.Identity, bias=round_up[:],
                                     scale=q_inv[:, i:i + 1]).then_inc(v_done, 1)

            def copy_qt(b, i):
                act.wait_ge(qt_done, NT * b + i + 1)
                nc.scalar.activation(qt[:], ps_qt[:].rearrange("p (c t) -> p c t", c=NC), ACT.Identity,
                                     bias=round_down[:]).then_inc(qt_copied, 1)

            def front(b, items, last):
                for off, k in items:
                    if not (last and off):
                        item(b + off, k)

            def batch(b, last):
                for s in range(SLOTS):
                    if 1 <= s <= NT:
                        square(b, s - 1)
                    if s >= 2:
                        quantise(b, s - 2)
                    front(b, FRONT_A[s], last)
                    if 1 <= s <= NT:
                        split_u(b, s - 1)
                    if s >= 2:
                        copy_qt(b, s - 2)
                    if HT <= s < NT:
                        front(b, FRONT_B[s], last)
                    if s + AHEAD < NT:
                        values_hi(b, s + AHEAD)
                    if s >= NT and not last:
                        values_hi(b + 1, s - NT)
                    if not HT <= s < NT:
                        front(b, FRONT_B[s], last)

            for k in range(NT):
                item(0, k)
            values_hi(0, 0)
            act.wait_ge(weight_in, 16)
            for k in range(NC):
                nc.scalar.activation(w_above[:, k, :], w_raw[:, k, :], ACT.Abs, accum_out=w_abs[:, k:k + 1]).then_inc(w_abs_done, 1)
            for k in range(NT, NT + HT):
                item(0, k)
                if k == NT:
                    values_hi(0, 1)
            for c in range(NC):
                act.wait_ge(wt_done, c + 1)
                nc.scalar.copy(w_t[:, c, :], ps_att[1][:]).then_inc(wt_copied, 1)
                if c in (1, 2):
                    item(0, NT + HT + c - 1)
            act.wait_ge(pool_const, 5)
            with act.Fori(0, B - 1) as b:
                batch(b, False)
            batch(B - 1, True)

        @block.vector
        def _(dve):
            def item(b, k):
                ps, hi, lo = item_parts(b, k)
                if has_diagonal(*ITEMS[k]):
                    dve.wait_ge(item_done, NI * b + k + 1)
                    nc.vector.tensor_tensor(ps[:, 0:P], ps[:, 0:P], mask[:], ALU.mult).then_inc(masked, 1)
                dve.wait_ge(item_hi, NI * b + k + 1)
                nc.vector.tensor_tensor(lo, ps, f32(hi), ALU.subtract).then_inc(item_lo, 1)

            def statistics(b, i):
                dve.wait_ge(x_in_sem[i], 16 * b + 16)
                nc.vector.bn_stats(bn[:, i, :], x_raw[:, i, :])

            def mean_variance(i):
                nc.vector.bn_aggr(mv[:, i, :], bn[:, i, :]).then_inc(mv_done, 1)

            def values(b, i):
                dve.wait_ge(rstd_done, NT * b + i + 1)
                if not (isinstance(b, int) and b == 0 and i < 2):
                    dve.wait_ge(q_lo_done, NT * b + i - 1)
                nc.vector.tensor_scalar(q_full[:, i % 2, :], x_raw[:, i, :], mv[:, i, 0:1], rstd[:, i:i + 1],
                                        ALU.subtract, ALU.mult).then_inc(q_done, 1)

            def residual(b, i):
                dve.wait_ge(att_done, NT * b + i + 1)
                nc.vector.scalar_tensor_tensor(out=z[:, i % 4, :], in0=ps_att[i % 2][:], scalar=1.0, in1=x_raw[:, i, :],
                                               op0=ALU.mult, op1=ALU.add,
                                               accum_out=z_sum[:, i:i + 1]).then_inc(z_done, 1)
                dve.wait_ge(z_done, NT * b + i + 1)
                nc.vector.tensor_scalar(z_mean[:, i, :], mean_scales[:], z_sum[:, i:i + 1], None,
                                        ALU.mult).then_inc(z_mean_done, 1)

            def first_chunk(b, i):
                dve.wait_ge(pairs_done, 2 * (NT * b + i) + 1)
                dve.wait_ge(z_mean_done, NT * b + i + 1)
                nc.vector.scalar_tensor_tensor(out=u[:, i % 2, 0, :], in0=pairs[:, i % 2, 0, :],
                                               scalar=z_mean[:, i, 1:2], in1=pairs[:, i % 2, 1, :],
                                               op0=ALU.subtract, op1=ALU.add).then_inc(u0_done, 1)

            def split_u(b, i):
                dve.wait_ge(ut_hi_done, NT * b + i + 1)
                nc.vector.tensor_tensor(ut_lo[:], ps_ut[:], f32(ut_hi[:]), ALU.subtract).then_inc(ut_lo_done, 1)

            def row_scale(b, i):
                at = slice(i, i + 1)
                dve.wait_ge(had_done, NT * b + i + 1)
                nc.vector.tensor_reduce(h_max[:, at], ps_had[:], AX_X, ALU.max,
                                        apply_absolute_value=True).then_inc(max_done, 1)
                dve.wait_ge(max_done, NT * b + i + 1)
                dve.wait_ge(z_rstd_done, NT * b + i + 1)
                nc.vector.tensor_scalar(h_top[:, at], h_max[:, at], z_rstd[:, at], QMIN, ALU.mult,
                                        ALU.max).then_inc(top_done, 1)
                dve.wait_ge(top_done, NT * b + i + 1)
                nc.vector.reciprocal(h_inv[:, at], h_top[:, at]).then_inc(inv_done, 1)
                nc.vector.tensor_scalar(q_scale[:, at], h_top[:, at], 1.0 / QPOS, None, ALU.mult)
                dve.wait_ge(inv_done, NT * b + i + 1)
                nc.vector.tensor_scalar(q_inv[:, at], h_inv[:, at], z_rstd[:, at], QPOS, ALU.mult,
                                        ALU.mult).then_inc(q_inv_done, 1)

            def clip(b, i):
                dve.wait_ge(v_done, NT * b + i + 1)
                nc.vector.tensor_scalar(v[:], v[:], ROUND + QNEG, ROUND + QPOS, ALU.max, ALU.min).then_inc(clipped, 1)

            def scale_ffn(b, i):
                dve.wait_ge(ffn_done, NT * b + i + 1)
                dve.wait_ge(stored[i % 4], 16 * (2 * b + i // 4))
                nc.vector.scalar_tensor_tensor(out=y[:, i % 4, :], in0=ps_ffn[:], scalar=q_scale[:, i:i + 1],
                                               in1=w_row[:], op0=ALU.mult, op1=ALU.mult).then_inc(y_scaled, 1)

            def front(b, items, last):
                for off, k in items:
                    if not (last and off):
                        item(b + off, k)

            def batch(b, last):
                for s in range(SLOTS):
                    i = s + AHEAD + 1
                    if s == 0:
                        statistics(b, i)
                        residual(b, s)
                    if s >= 2:
                        row_scale(b, s - 2)
                    if 1 <= s <= NT:
                        first_chunk(b, s - 1)
                    if 0 < s and i < NT:
                        statistics(b, i)
                    elif 0 < s < NT and not last:
                        statistics(b + 1, i - NT)
                    if 2 <= s < SLOTS - 1:
                        clip(b, s - 2)
                    front(b, FRONT_A[s], last)
                    if s == SLOTS - 1:
                        clip(b, s - 2)
                    if 1 <= s <= NT:
                        split_u(b, s - 1)
                    if s + AHEAD < NT:
                        values(b, s + AHEAD)
                    if s >= NT and not last:
                        values(b + 1, s - NT)
                    front(b, FRONT_B[s], last)
                    if 0 < s < NT:
                        residual(b, s)
                    if i < NT or (s < NT and not last):
                        mean_variance(i % NT)
                    if s >= 2:
                        scale_ffn(b, s - 2)

            nc.vector.memset(mean_scales[:, 0:1], -1.0 / D)
            nc.vector.memset(mean_scales[:, 1:2], NC / D)
            nc.vector.memset(ones[:], 1.0)
            for k in range(4):
                item(0, k)
            dve.wait_ge(x_in_sem[0], 16)
            nc.vector.bn_stats(bn[:, 0, :], x_raw[:, 0, :]).then_inc(bn_done, 1)
            dve.wait_ge(bn_done, 1)
            mean_variance(0)
            for k in range(4, NT):
                item(0, k)
            dve.wait_ge(ident_in_sem, 16)
            dve.wait_ge(const_in, CONSTS)
            nc.vector.tensor_copy(ident_r[:], ident[:]).then_inc(dve_const, 1)
            nc.vector.tensor_copy(had_r[:], had[:]).then_inc(dve_const, 1)
            values(0, 0)
            for i in range(1, AHEAD + 1):
                dve.wait_ge(x_in_sem[i], 16)
                nc.vector.bn_stats(bn[:, i, :], x_raw[:, i, :]).then_inc(bn_done, 1)
                dve.wait_ge(bn_done, i + 1)
                mean_variance(i)
            dve.wait_ge(w_abs_done, NC)
            nc.vector.tensor_scalar(w_scale[:], w_abs[:], 1.0 / D, QMIN, ALU.mult, ALU.max).then_inc(w_step, 1)
            dve.wait_ge(w_step, 1)
            nc.vector.tensor_scalar(w_thr[:], w_scale[:], 0.5, None, ALU.mult).then_inc(w_step, 1)
            nc.vector.tensor_scalar(w_nthr[:], w_scale[:], -0.5, None, ALU.mult).then_inc(w_step, 1)
            for k in range(NC):
                nc.vector.tensor_scalar(w_diag[:, k, :], ident[:], w_scale[:, k:k + 1], None, ALU.mult).then_inc(w_step, 1)
            dve.wait_ge(w_step, 3)
            for k in range(NC):
                nc.vector.tensor_scalar(w_below[:, k, :], w_raw[:, k, :], w_nthr[:, k:k + 1], None, ALU.is_lt).then_inc(w_cmp, 1)
            for k in range(NC):
                item(0, NT + k)
                if k == 0:
                    values(0, 1)
                dve.wait_ge(w_cmp, k + 1)
                nc.vector.scalar_tensor_tensor(out=w_tern[:, k, :], in0=w_raw[:, k, :], scalar=w_thr[:, k:k + 1],
                                               in1=w_below[:, k, :], op0=ALU.is_gt, op1=ALU.subtract).then_inc(w_tern_done, 1)
            for k in range(NT + NC, EARLY):
                item(0, k)
            dve.wait_ge(w_row_sum, 1)
            nc.vector.tensor_copy(w_row[:], ps_ffn[:]).then_inc(w_row_done, 1)
            dve.wait_ge(w_row_done, 1)
            with dve.Fori(0, B - 1) as b:
                batch(b, False)
            batch(B - 1, True)

        @block.gpsimd
        def _(pool):
            def norm(b, i):
                at = slice(i, i + 1)
                pool.wait_ge(mv_done, NT * b + i + 1)
                nc.gpsimd.tensor_tensor(var_eps[:, at], mv[:, i, 1:2], eps[:, 0:1], ALU.add).then_inc(var_eps_done, 1)
                pool.wait_ge(var_eps_done, NT * b + i + 1)
                nc.gpsimd.tensor_tensor(rstd[:, at], var_eps[:, at], minus_half[:], ALU.pow).then_inc(rstd_done, 1)

            def values_lo(b, i):
                pool.wait_ge(q_hi_done, NT * b + i + 1)
                nc.gpsimd.tensor_tensor(q_lo[:, i, :], q_full[:, i % 2, :], f32(q_hi[:, i, :]),
                                        ALU.subtract).then_inc(q_lo_done, 1)

            def butterflies(b, i):
                r = i % 2
                pool.wait_ge(z_done, NT * b + i + 1)
                lower, upper = z[:, i % 4, 0:2 * P], z[:, i % 4, 2 * P:4 * P]
                p = pairs[:, r, :, :].rearrange("p c t -> p (c t)")
                nc.gpsimd.tensor_tensor(p[:, 0:2 * P], lower, upper, ALU.add).then_inc(pairs_done, 1)
                nc.gpsimd.tensor_tensor(p[:, 2 * P:4 * P], lower, upper, ALU.subtract).then_inc(pairs_done, 1)
                pool.wait_ge(pairs_done, 2 * (NT * b + i) + 2)
                nc.gpsimd.tensor_tensor(u[:, r, 2, :], pairs[:, r, 2, :], pairs[:, r, 3, :], ALU.add)
                both = pairs[:, r, :, :].rearrange("p (g h) t -> p g h t", h=2)
                to = u[:, r, :, :].rearrange("p (g h) t -> p g h t", h=2)
                nc.gpsimd.tensor_tensor(to[:, :, 1, :], both[:, :, 0, :], both[:, :, 1, :], ALU.subtract).then_inc(u_done, 1)

            def norm_z(b, i):
                at = slice(i, i + 1)
                pool.wait_ge(sq_done, NT * b + i + 1)
                nc.gpsimd.tensor_tensor(z_sq_eps[:, at], z_sq[:, at], eps[:, 1:2], ALU.add).then_inc(z_eps_done, 1)
                pool.wait_ge(z_eps_done, NT * b + i + 1)
                nc.gpsimd.tensor_tensor(z_rstd[:, at], z_sq_eps[:, at], minus_half[:], ALU.pow).then_inc(z_rstd_done, 1)

            def add_z(b, i):
                pool.wait_ge(y_scaled, NT * b + i + 1)
                nc.gpsimd.tensor_tensor(y[:, i % 4, :], y[:, i % 4, :], z[:, i % 4, :], ALU.add).then_inc(y_done, 1)

            def batch(b, last):
                for s in range(SLOTS):
                    if 1 <= s <= NT:
                        butterflies(b, s - 1)
                        norm_z(b, s - 1)
                    if s + AHEAD < NT:
                        norm(b, s + AHEAD)
                    if s >= NT and not last:
                        norm(b + 1, s - NT)
                    if s + 1 < NT:
                        values_lo(b, s + 1)
                    if s == SLOTS - 1 and not last:
                        values_lo(b + 1, 0)
                    if s >= 3:
                        add_z(b, s - 3)
                add_z(b, NT - 1)

            nc.gpsimd.memset(minus_half[:], -0.5).then_inc(pool_const, 1)
            nc.gpsimd.memset(round_up[:], ROUND).then_inc(pool_const, 1)
            nc.gpsimd.memset(round_down[:], -ROUND).then_inc(pool_const, 1)
            nc.gpsimd.memset(eps[:, 0:1], EPS).then_inc(pool_const, 1)
            nc.gpsimd.memset(eps[:, 1:2], D * EPS).then_inc(pool_const, 1)
            pool.wait_ge(pool_const, 5)
            norm(0, 0)
            values_lo(0, 0)
            norm(0, 1)
            with pool.Fori(0, B - 1) as b:
                batch(b, False)
            batch(B - 1, True)


def kernel(x, ctx_1024, L0_ffn_weight):
    import numpy as np
    import concourse.bacc as bacc
    from concourse import mybir as mb
    from concourse.bass_utils import run_bass_kernel_spmd

    had = np.ones((1, 1), np.float32)
    while had.shape[0] < P:
        had = np.block([[had, had], [had, -had]])
    arrays = {
        "x_dram": np.ascontiguousarray(x),
        "ctx_dram": np.ascontiguousarray(ctx_1024),
        "weight_dram": np.ascontiguousarray(L0_ffn_weight),
        "ident_dram": np.eye(P, dtype=np.float32),
        "had_dram": np.ascontiguousarray(had, dtype=np.float32),
        "mask_dram": np.triu(np.ones((P, P), np.float32)),
    }
    nc = bacc.Bacc("TRN2", target_bir_lowering=False, num_devices=1)
    args = [nc.dram_tensor(n, a.shape, mb.dt.from_np(a.dtype), kind="ExternalInput").ap() for n, a in arrays.items()]
    out = nc.dram_tensor("out_dram", (B, L, D), mb.dt.float32, kind="ExternalOutput").ap()
    build(nc, *args, out)
    r = run_bass_kernel_spmd(nc, [arrays], core_ids=[0])
    return r.results[0]["out_dram"]
```

```python
from contextlib import ExitStack

import concourse.bass as bass
from concourse import mybir

ALU = mybir.AluOpType
ACT = mybir.ActivationFunctionType
AX_X = mybir.AxisListType.X
F32 = mybir.dt.float32
F32R = mybir.dt.float32r
BF16 = mybir.dt.bfloat16

P = 128
B, L, D = 4, 1024, 512
NT = L // P
NC = D // P
HD = D // 2
HALF = L // 2
HT = NT // 2
EPS = 1e-5
QPOS, QNEG = 7.0, -8.0
QMIN = 1e-5
ROUND = 1.5 * 2.0**23

CONSTS = 3 * 16

ITEMS = ([(j, P * j, HALF) for j in range(HT - 1)] + [(HT - 1, HALF - P, HALF + P)]
         + [(j, HALF, L) for j in range(HT - 1)] + [(HT - 1, HALF + P, L)] + [(j, P * j, L) for j in range(HT, NT)])
NI = len(ITEMS)
SLOTS = NT + 2
FRONT_A = [[(0, 5), (0, 6)], [(0, 7)], [(0, 9)], [(0, 10)], [(0, 11)], [], [], [],
           [(1, 0)], [(1, 2), (1, 3)]]
FRONT_B = [[], [(0, 8)], [], [], [], [], [], [],
           [(1, 1)], [(1, 4)]]
EARLY = 5
UNITS = [[], [], [0], [1], [2], [3, 4], [5, 6], [7], [], []]
POOL_UNITS = (4, 5)
NU = 2 * NC
AHEAD = 2
STATS_AHEAD = 4
CUTS = (5, 3)


def item_base(k):
    return sum(end - first for _, first, end in ITEMS[:k])


def item_of_tile(j, i):
    return next(k for k, (key, first, end) in enumerate(ITEMS) if key == j and first <= P * i < end)


def has_diagonal(k):
    return ITEMS[k][1] == P * ITEMS[k][0]


def diagonals_before(b, k):
    return NT * b + sum(has_diagonal(i) for i in range(k))


def build(nc, x_in, ctx_in, w_in, ident_in, had_in, mask_in, out):
    with ExitStack() as stack:
        def sb(name, shape, dt=F32):
            return stack.enter_context(nc.sbuf_tensor(name, shape, dt))

        def sem(name):
            return stack.enter_context(nc.semaphore(name))

        def bank(name):
            return stack.enter_context(nc.psum_tensor(name, [P, D], F32))

        ps_item = [bank(f"ps_item{i}") for i in range(2)]
        ps_att = [bank(f"ps_att{i}") for i in range(2)]
        ps_ut = bank("ps_ut")
        ps_had = bank("ps_had")
        ps_qt = stack.enter_context(nc.psum_tensor("ps_qt", [P, 2 * D], BF16))
        ps_ffn = bank("ps_ffn")

        ident = sb("ident", [P, P])
        ident_b = sb("ident_b", [P, P], BF16)
        had = sb("had", [P, P])
        had_r = sb("had_r", [P, 2, 2 * P], F32R)
        mask = sb("mask", [P, P])
        mean_scales = sb("mean_scales", [P, 2])
        minus_half = sb("minus_half", [P, 1])
        round_up = sb("round_up", [P, 1])
        eps = sb("eps", [P, 2])
        ones = sb("ones", [P, P])
        w_raw = sb("w_raw", [P, NC, D])
        w_abs = sb("w_abs", [P, NC])
        w_scale = sb("w_scale", [P, NC])
        w_thr = sb("w_thr", [P, NC])
        w_nthr = sb("w_nthr", [P, NC])
        w_below = sb("w_below", [P, NC, D], BF16)
        w_tern = sb("w_tern", [P, NC, D], BF16)
        w_diag = sb("w_diag", [P, NC, P])
        w_t = sb("w_t", [P, NC, D], BF16)
        w_row = sb("w_row", [P, D])

        kt_raw = sb("kt_raw", [P, NC, L])
        kt_hi = sb("kt_hi", [P, NC, L], F32R)
        kt_lo = sb("kt_lo", [P, NC, L], F32R)
        x_raw = sb("x_raw", [P, NT, D])
        q_hi = sb("q_hi", [P, NT, D], F32R)
        q_lo = sb("q_lo", [P, NT, D], F32R)
        a_hi = sb("a_hi", [P, item_base(NI)], F32R)
        a_lo = sb("a_lo", [P, item_base(NI)], F32R)

        q_full = sb("q_full", [P, 2, D])
        z = sb("z", [P, 4, D])
        u = sb("u", [P, 2, D])
        ut_hi = sb("ut_hi", [P, D], F32R)
        ut_lo = sb("ut_lo", [P, D], F32R)
        junk = sb("junk", [P, D])
        v = sb("v", [P, D])
        q_int = sb("q_int", [P, D], BF16)
        qt = sb("qt", [P, NC, P], BF16)
        y = sb("y", [P, 4, D])

        bn = sb("bn", [P, NT, 6])
        mv = sb("mv", [P, NT, 2])
        var_eps = sb("var_eps", [P, NT])
        rstd = sb("rstd", [P, NT])
        z_sum = sb("z_sum", [P, NT])
        z_mean = sb("z_mean", [P, NT, 2])
        z_sq = sb("z_sq", [P, NT])
        z_sq_eps = sb("z_sq_eps", [P, NT])
        z_rstd = sb("z_rstd", [P, NT])
        h_max = sb("h_max", [P, NT])
        h_top = sb("h_top", [P, NT])
        h_inv = sb("h_inv", [P, NT])
        q_inv = sb("q_inv", [P, NT])
        q_scale = sb("q_scale", [P, NT])

        const_in = sem("const_in")
        weight_in = [sem(f"weight_in{k}") for k in range(NC)]
        kt_in = [sem(f"kt_in{n}") for n in range(NU)]
        x_in_sem = [sem(f"x_in{j}") for j in range(NT)]
        stored = [sem(f"stored{i}") for i in range(4)]
        item_done = sem("item_done")
        att_done = sem("att_done")
        ut_done = sem("ut_done")
        had_done = sem("had_done")
        qt_done = sem("qt_done")
        ffn_done = sem("ffn_done")
        wt_done = sem("wt_done")
        w_row_sum = sem("w_row_sum")
        kt_hi_done = sem("kt_hi_done")
        w_abs_done = sem("w_abs_done")
        w_diag_done = sem("w_diag_done")
        item_hi = sem("item_hi")
        q_hi_done = sem("q_hi_done")
        sq_done = sem("sq_done")
        ut_hi_done = sem("ut_hi_done")
        v_done = sem("v_done")
        had_r_done = sem("had_r_done")
        ones_done = sem("ones_done")
        ident_b_done = sem("ident_b_done")
        kt_lo_done = [sem(f"kt_lo_done{half}") for half in range(2)]
        masked = sem("masked")
        item_lo = sem("item_lo")
        bn_done = sem("bn_done")
        mv_done = sem("mv_done")
        q_done = sem("q_done")
        z_done = sem("z_done")
        z_mean_done = sem("z_mean_done")
        lower_done = sem("lower_done")
        ut_lo_done = sem("ut_lo_done")
        max_done = sem("max_done")
        top_done = sem("top_done")
        inv_done = sem("inv_done")
        q_inv_done = sem("q_inv_done")
        clipped = sem("clipped")
        qt_copied = sem("qt_copied")
        y_scaled = sem("y_scaled")
        last_y_done = sem("last_y_done")
        w_scale_done = sem("w_scale_done")
        w_thr_done = sem("w_thr_done")
        w_below_done = sem("w_below_done")
        w_tern_done = sem("w_tern_done")
        pool_const = sem("pool_const")
        var_eps_done = sem("var_eps_done")
        rstd_done = sem("rstd_done")
        q_lo_done = sem("q_lo_done")
        x_sum_done = sem("x_sum_done")
        upper_done = sem("upper_done")
        z_eps_done = sem("z_eps_done")
        z_rstd_done = sem("z_rstd_done")
        y_done = sem("y_done")

        kt_chunks = ctx_in.rearrange("b (c p) t -> p (b c) t", p=P)
        w_rows = w_in.rearrange("(k p) i -> p k i", p=P)
        x_rows = x_in.rearrange("b (j p) d -> p (b j) d", p=P)
        out_rows = out.rearrange("b (j p) d -> p (b j) d", p=P)

        def f32(ap):
            return ap.bitcast(F32)

        def unit(n):
            half, c = divmod(n, NC)
            return c, slice(HALF * half, HALF * half + HALF)

        def item_parts(k):
            _, first, end = ITEMS[k]
            cols = slice(item_base(k), item_base(k + 1))
            return ps_item[k % 2][:, 0:end - first], a_hi[:, cols], a_lo[:, cols]

        def had_bank(b, i):
            return ps_item[0] if isinstance(b, int) and (b, i) == (B - 1, NT - 1) else ps_had

        wt_banks = [ps_qt[:], ps_had[:].bitcast(BF16)]

        block = stack.enter_context(nc.Block())

        @block.sync
        def _(sp):
            def load_kt(b, n):
                c, rows = unit(n)
                sp.dma_start(kt_raw[:, c:c + 1, rows], kt_chunks[:, bass.ds(NC * b + c, 1), rows]).then_inc(kt_in[n], 16)

            def load_x(b, j):
                sp.dma_start(x_raw[:, j:j + 1, :], x_rows[:, bass.ds(NT * b + j, 1), :]).then_inc(x_in_sem[j], 16)

            def batch(b, last):
                for s in range(SLOTS):
                    if not last and s < 2:
                        sp.wait_ge(kt_lo_done[s], NC * b + NC)
                        for n in range(NC * s, NC * s + NC):
                            load_kt(b + 1, n)
                    if not last and s < NT:
                        sp.wait_ge(z_done, NT * b + s + 1)
                        load_x(b + 1, s)
                    if s >= 3:
                        i = s - 3
                        sp.wait_ge(y_done, NT * b + i + 1)
                        sp.dma_start(out_rows[:, bass.ds(NT * b + i, 1), :], y[:, i % 4:i % 4 + 1, :]).then_inc(
                            stored[i % 4], 16)
                i = NT - 1
                if last:
                    sp.wait_ge(last_y_done, 1)
                else:
                    sp.wait_ge(y_done, NT * b + i + 1)
                sp.dma_start(out_rows[:, bass.ds(NT * b + i, 1), :], y[:, i % 4:i % 4 + 1, :]).then_inc(
                    stored[i % 4], 16)

            def load_w(k):
                sp.dma_start(w_raw[:, k:k + 1, :], w_rows[:, k:k + 1, :]).then_inc(weight_in[k], 16)

            for n in range(NC):
                load_kt(0, n)
            sp.dma_start(ident[:], ident_in).then_inc(const_in, 16)
            sp.dma_start(had[:], had_in).then_inc(const_in, 16)
            sp.dma_start(mask[:], mask_in).then_inc(const_in, 16)
            load_x(0, 0)
            for k in range(2):
                load_w(k)
            for n in range(NC, NU):
                load_kt(0, n)
            for k in range(2, NC):
                load_w(k)
            for j in range(1, NT):
                load_x(0, j)
            with sp.Fori(0, B - 1) as b:
                batch(b, False)
            batch(B - 1, True)
            for i in range(4):
                sp.wait_ge(stored[i], 16 * B * NT // 4)

        @block.tensor
        def _(pe):
            def item(b, k):
                j, first, end = ITEMS[k]
                ps = ps_item[k % 2]
                at_start = isinstance(b, int) and b == 0
                if not (at_start and k == 0):
                    pe.wait_ge(kt_lo_done[0], NC * b + NC)
                if end > HALF:
                    pe.wait_ge(kt_lo_done[1], NC * b + NC)
                if not (at_start and k < 2):
                    pe.wait_ge(item_lo, NI * b + k - 1)
                n = end - first
                steps = [(c, l, r) for l, r in ((kt_hi, kt_hi), (kt_hi, kt_lo), (kt_lo, kt_hi)) for c in range(NC)]
                for n_step, (c, l, r) in enumerate(steps):
                    if at_start and k == 0 and n_step < NC:
                        pe.wait_ge(kt_hi_done, c + 1)
                    elif at_start and k == 0 and n_step < 2 * NC:
                        pe.wait_ge(kt_lo_done[0], c + 1)
                    last = nc.tensor.matmul(ps[:, 0:n], l[:, c, P * j:P * j + P], r[:, c, first:end],
                                            start=(n_step == 0), stop=(n_step == len(steps) - 1))
                last.then_inc(item_done, 1)

            def attention(b, i, steps):
                if steps[0] == 0:
                    pe.wait_ge(item_lo, NI * b + max(item_of_tile(j, i) for j in range(i + 1)) + 1)
                    pe.wait_ge(q_lo_done, NT * b + i + 1)
                    pe.wait_ge(q_hi_done, NT * b + i + 1)
                for n in range(*steps):
                    j = n // 3
                    k = item_of_tile(j, i)
                    at = item_base(k) + P * i - ITEMS[k][1]
                    l, r = ((a_hi, q_hi), (a_hi, q_lo), (a_lo, q_hi))[n % 3]
                    last = nc.tensor.matmul(ps_att[i % 2][:], l[:, at:at + P], r[:, j, :],
                                            start=(n == 0), stop=(n == 3 * i + 2))
                if n == 3 * i + 2:
                    last.then_inc(att_done, 1)

            def transpose_u(b, i):
                pe.wait_ge(upper_done, NT * b + i + 1)
                pe.wait_ge(lower_done, NT * b + i + 1)
                for c in range(NC):
                    last = nc.tensor.transpose(ps_ut[:, P * c:P * c + P], u[:, i % 2, P * c:P * c + P], ident[:])
                last.then_inc(ut_done, 1)

            def hadamard(b, i):
                pe.wait_ge(ut_lo_done, NT * b + i + 1)
                for half in range(2):
                    out_cols = slice(2 * P * half, 2 * P * half + 2 * P)
                    for c in range(2):
                        cols = slice(P * (2 * half + c), P * (2 * half + c) + P)
                        nc.tensor.matmul(had_bank(b, i)[:, out_cols], ut_hi[:, cols], had_r[:, c, :], start=(c == 0), stop=False)
                        last = nc.tensor.matmul(had_bank(b, i)[:, out_cols], ut_lo[:, cols], had_r[:, c, :], start=False,
                                                stop=(c == 1))
                last.then_inc(had_done, 1)

            def transpose_q(b, i):
                pe.wait_ge(clipped, NT * b + i + 1)
                for c in range(NC):
                    last = nc.tensor.transpose(ps_qt[:, P * c:P * c + P], q_int[:, P * c:P * c + P], ident_b[:])
                last.then_inc(qt_done, 1)

            def ffn(b, i):
                pe.wait_ge(qt_copied, NT * b + i + 1)
                pe.wait_ge(y_scaled, NT * b + i)
                for c in range(NC):
                    last = nc.tensor.matmul(ps_ffn[:], qt[:, c, :], w_t[:, c, :], start=(c == 0), stop=(c == NC - 1))
                last.then_inc(ffn_done, 1)

            def front(b, items, last):
                for off, k in items:
                    if not (last and off):
                        item(b + off, k)

            def batch(b, last):
                for s in range(SLOTS):
                    total = 3 * (s + 1)
                    cuts = (total - sum(CUTS), total - CUTS[1], total) if 2 <= s < NT else (total, total, total)
                    if s == 0:
                        attention(b, s, (0, total))
                    front(b, FRONT_A[s], last)
                    if 0 < s < NT:
                        attention(b, s, (0, cuts[0]))
                    if 1 <= s <= NT:
                        transpose_u(b, s - 1)
                    if s == NT and last:
                        hadamard(b, s - 1)
                    if 2 <= s < NT:
                        attention(b, s, (cuts[0], cuts[1]))
                    if s >= 2:
                        transpose_q(b, s - 2)
                    if 2 <= s < NT:
                        attention(b, s, (cuts[1], cuts[2]))
                    front(b, FRONT_B[s], last)
                    if 1 <= s < NT or (s == NT and not last):
                        hadamard(b, s - 1)
                    if s >= 2:
                        ffn(b, s - 2)

            for k in range(EARLY):
                item(0, k)
            pe.wait_ge(const_in, CONSTS)
            pe.wait_ge(ident_b_done, 1)
            pe.wait_ge(w_tern_done, NC)
            for c in range(NC):
                for k in range(NC):
                    last = nc.tensor.transpose(wt_banks[c // 2][:, D * (c % 2) + P * k:D * (c % 2) + P * k + P],
                                               w_tern[:, k, P * c:P * c + P], ident_b[:])
                if c % 2:
                    last.then_inc(wt_done, 1)
            pe.wait_ge(w_diag_done, NC)
            pe.wait_ge(ones_done, 1)
            for k in range(NC):
                last = nc.tensor.matmul(ps_ffn[:, P * k:P * k + P], ones[:], w_diag[:, k, :], start=True, stop=True)
            last.then_inc(w_row_sum, 1)
            pe.wait_ge(had_r_done, 4)
            with pe.Fori(0, B - 1) as b:
                batch(b, False)
            batch(B - 1, True)

        @block.scalar
        def _(act):
            def split_kt(b, n):
                c, rows = unit(n)
                if not (isinstance(b, int) and b == 0):
                    act.wait_ge(item_done, NI * (b - 1) + (NI if n >= NC else NI - HT))
                act.wait_ge(kt_in[n], 16 * b + 16)
                nc.scalar.copy(kt_hi[:, c, rows], kt_raw[:, c, rows]).then_inc(kt_hi_done, 1)

            def item(b, k):
                ps, hi, _ = item_parts(k)
                if has_diagonal(k):
                    act.wait_ge(masked, diagonals_before(b, k) + 1)
                else:
                    act.wait_ge(item_done, NI * b + k + 1)
                nc.scalar.copy(hi, ps).then_inc(item_hi, 1)

            def values_hi(b, i):
                act.wait_ge(q_done, NT * b + i + 1)
                nc.scalar.copy(q_hi[:, i, :], q_full[:, i % 2, :]).then_inc(q_hi_done, 1)

            def square(b, i):
                act.wait_ge(z_mean_done, NT * b + i + 1)
                nc.scalar.activation(junk[:], z[:, i % 4, :], ACT.Square, bias=z_mean[:, i, 0:1],
                                     accum_out=z_sq[:, i:i + 1]).then_inc(sq_done, 1)

            def split_u(b, i):
                act.wait_ge(ut_done, NT * b + i + 1)
                nc.scalar.copy(ut_hi[:], ps_ut[:]).then_inc(ut_hi_done, 1)

            def quantise(b, i):
                act.wait_ge(q_inv_done, NT * b + i + 1)
                nc.scalar.activation(v[:], had_bank(b, i)[:], ACT.Identity, bias=round_up[:],
                                     scale=q_inv[:, i:i + 1]).then_inc(v_done, 1)

            def front(b, items, last):
                for off, k in items:
                    if not (last and off):
                        item(b + off, k)

            def batch(b, last):
                for s in range(SLOTS):
                    if 1 <= s <= NT:
                        square(b, s - 1)
                    if s == NT and last:
                        split_u(b, s - 1)
                    if s >= 2:
                        quantise(b, s - 2)
                    front(b, FRONT_A[s], last)
                    if 1 <= s < NT or (s == NT and not last):
                        split_u(b, s - 1)
                    if not last:
                        for n in UNITS[s]:
                            split_kt(b + 1, n)
                    if s + AHEAD < NT:
                        values_hi(b, s + AHEAD)
                    if s >= NT and not last:
                        values_hi(b + 1, s - NT)
                    front(b, FRONT_B[s], last)

            for n in range(NC):
                split_kt(0, n)
            act.wait_ge(const_in, CONSTS)
            for at, sign in ((had_r[:, 0, 0:P], 1.0), (had_r[:, 0, P:2 * P], 1.0), (had_r[:, 1, 0:P], 1.0),
                             (had_r[:, 1, P:2 * P], -1.0)):
                nc.scalar.activation(at, had[:], ACT.Copy, scale=sign).then_inc(had_r_done, 1)
            def weight_sum(k):
                act.wait_ge(weight_in[k], 16)
                nc.scalar.activation(w_below[:, k, :], w_raw[:, k, :], ACT.Abs, accum_out=w_abs[:, k:k + 1]).then_inc(w_abs_done, 1)

            weight_sum(0)
            weight_sum(1)
            split_kt(0, NC)
            split_kt(0, NC + 1)
            item(0, 0)
            split_kt(0, NC + 2)
            split_kt(0, NC + 3)
            weight_sum(2)
            item(0, 1)
            weight_sum(3)
            item(0, 2)
            values_hi(0, 0)
            act.wait_ge(w_scale_done, NC)
            for k in range(NC):
                nc.scalar.mul(w_diag[:, k, :], ident[:], w_scale[:, k:k + 1]).then_inc(w_diag_done, 1)
            item(0, 3)
            item(0, 4)
            values_hi(0, 1)
            for half in range(2):
                act.wait_ge(wt_done, half + 1)
                nc.scalar.copy(w_t[:, 2 * half:2 * half + 2, :].rearrange("p c o -> p (c o)"), wt_banks[half])
            act.wait_ge(w_row_sum, 1)
            nc.scalar.copy(w_row[:], ps_ffn[:])
            act.wait_ge(pool_const, 4)
            with act.Fori(0, B - 1) as b:
                batch(b, False)
            batch(B - 1, True)

        @block.vector
        def _(dve):
            def split_kt(b, n):
                c, rows = unit(n)
                dve.wait_ge(kt_hi_done, NU * b + n + 1)
                nc.vector.tensor_tensor(kt_lo[:, c, rows], kt_raw[:, c, rows], f32(kt_hi[:, c, rows]),
                                        ALU.subtract).then_inc(kt_lo_done[n // NC], 1)

            def mask_item(b, k):
                if has_diagonal(k):
                    ps = item_parts(k)[0]
                    dve.wait_ge(item_done, NI * b + k + 1)
                    nc.vector.tensor_tensor(ps[:, 0:P], ps[:, 0:P], mask[:], ALU.mult).then_inc(masked, 1)

            def split_item(b, k):
                ps, hi, lo = item_parts(k)
                dve.wait_ge(item_hi, NI * b + k + 1)
                nc.vector.tensor_tensor(lo, ps, f32(hi), ALU.subtract).then_inc(item_lo, 1)

            def item(b, k):
                mask_item(b, k)
                split_item(b, k)

            def statistics(b, i):
                dve.wait_ge(x_in_sem[i], 16 * b + 16)
                nc.vector.bn_stats(bn[:, i, :], x_raw[:, i, :])

            def mean_variance(i):
                nc.vector.bn_aggr(mv[:, i, :], bn[:, i, :]).then_inc(mv_done, 1)

            def values(b, i):
                dve.wait_ge(rstd_done, NT * b + i + 1)
                if not (isinstance(b, int) and b == 0 and i < 2):
                    dve.wait_ge(x_sum_done, NT * b + i - 1)
                nc.vector.tensor_scalar(q_full[:, i % 2, :], x_raw[:, i, :], mv[:, i, 0:1], rstd[:, i:i + 1],
                                        ALU.subtract, ALU.mult).then_inc(q_done, 1)

            def residual(b, i):
                dve.wait_ge(att_done, NT * b + i + 1)
                dve.wait_ge(x_sum_done, NT * b + i + 1)
                nc.vector.scalar_tensor_tensor(out=z[:, i % 4, :], in0=ps_att[i % 2][:], scalar=1.0, in1=x_raw[:, i, :],
                                               op0=ALU.mult, op1=ALU.add,
                                               accum_out=z_sum[:, i:i + 1]).then_inc(z_done, 1)

            def means(b, i):
                dve.wait_ge(z_done, NT * b + i + 1)
                nc.vector.tensor_scalar(z_mean[:, i, :], mean_scales[:], z_sum[:, i:i + 1], None,
                                        ALU.mult).then_inc(z_mean_done, 1)

            def lower_half(b, i):
                dve.wait_ge(z_mean_done, NT * b + i + 1)
                nc.vector.scalar_tensor_tensor(out=u[:, i % 2, 0:HD], in0=z[:, i % 4, 0:HD],
                                               scalar=z_mean[:, i, 1:2], in1=z[:, i % 4, HD:D],
                                               op0=ALU.subtract, op1=ALU.add).then_inc(lower_done, 1)

            def split_u(b, i):
                dve.wait_ge(ut_hi_done, NT * b + i + 1)
                nc.vector.tensor_tensor(ut_lo[:], ps_ut[:], f32(ut_hi[:]), ALU.subtract).then_inc(ut_lo_done, 1)

            def row_scale(b, i):
                at = slice(i, i + 1)
                dve.wait_ge(had_done, NT * b + i + 1)
                nc.vector.tensor_reduce(h_max[:, at], had_bank(b, i)[:], AX_X, ALU.max,
                                        apply_absolute_value=True).then_inc(max_done, 1)
                dve.wait_ge(max_done, NT * b + i + 1)
                dve.wait_ge(z_rstd_done, NT * b + i + 1)
                nc.vector.tensor_scalar(h_top[:, at], h_max[:, at], z_rstd[:, at], QMIN, ALU.mult,
                                        ALU.max).then_inc(top_done, 1)
                dve.wait_ge(top_done, NT * b + i + 1)
                nc.vector.reciprocal(h_inv[:, at], h_top[:, at]).then_inc(inv_done, 1)
                nc.vector.tensor_scalar(q_scale[:, at], h_top[:, at], 1.0 / QPOS, None, ALU.mult)
                dve.wait_ge(inv_done, NT * b + i + 1)
                nc.vector.tensor_scalar(q_inv[:, at], h_inv[:, at], z_rstd[:, at], QPOS, ALU.mult,
                                        ALU.mult).then_inc(q_inv_done, 1)

            def clip(b, i):
                dve.wait_ge(v_done, NT * b + i + 1)
                nc.vector.tensor_scalar(q_int[:], v[:], ROUND, QPOS, ALU.subtract, ALU.min).then_inc(clipped, 1)

            def copy_qt(b, i):
                dve.wait_ge(qt_done, NT * b + i + 1)
                nc.vector.tensor_scalar(qt[:], ps_qt[:, 0:D].rearrange("p (c t) -> p c t", c=NC), QNEG, None,
                                        ALU.max).then_inc(qt_copied, 1)

            def scale_ffn(b, i):
                dve.wait_ge(ffn_done, NT * b + i + 1)
                dve.wait_ge(stored[i % 4], 16 * (2 * b + i // 4))
                nc.vector.scalar_tensor_tensor(out=y[:, i % 4, :], in0=ps_ffn[:], scalar=q_scale[:, i:i + 1],
                                               in1=w_row[:], op0=ALU.mult, op1=ALU.mult).then_inc(y_scaled, 1)

            def front(b, items, last):
                for off, k in items:
                    if not (last and off):
                        item(b + off, k)

            late_item = FRONT_B[NT][0][1]

            def batch(b, last):
                for s in range(SLOTS):
                    i = s + STATS_AHEAD
                    final = s == SLOTS - 1
                    items = [(b + off, k) for off, k in FRONT_A[s] if not (last and off)]
                    if s == 0:
                        residual(b, s)
                        statistics(b, i)
                        means(b, s)
                        values(b, s + AHEAD)
                        lower_half(b, s)
                    if s >= 2:
                        row_scale(b, s - 2)
                    if final and not last:
                        split_item(b + 1, late_item)
                    if s < NT:
                        for front_item in items:
                            mask_item(*front_item)
                    elif final and items:
                        mask_item(*items[0])
                    if s and not last:
                        for n in UNITS[s - 1]:
                            if n not in POOL_UNITS:
                                split_kt(b + 1, n)
                    if s == NT and last:
                        split_u(b, s - 1)
                    if s >= 2:
                        clip(b, s - 2)
                    if s == NT and items:
                        mask_item(*items[0])
                    if s in (NT - 1, NT):
                        scale_ffn(b, s - 3)
                    for n_item, front_item in enumerate(items):
                        if final and n_item:
                            mask_item(*front_item)
                        split_item(*front_item)
                    if final:
                        scale_ffn(b, s - 3)
                    if s == 1:
                        residual(b, s)
                        means(b, s)
                    if 1 <= s < NT or (s == NT and not last):
                        split_u(b, s - 1)
                    if s >= 2:
                        copy_qt(b, s - 2)
                    if 3 <= s < NT - 1:
                        scale_ffn(b, s - 3)
                    if 2 <= s < NT:
                        residual(b, s)
                    if 0 < s and i < NT:
                        statistics(b, i)
                    elif 0 < s < NT and not last:
                        statistics(b + 1, i - NT)
                    if 2 <= s < NT:
                        means(b, s)
                    if 0 < s and s + AHEAD < NT:
                        values(b, s + AHEAD)
                    if s >= NT and not last:
                        values(b + 1, s - NT)
                    if 0 < s < NT:
                        lower_half(b, s)
                    if s == NT and not last:
                        mask_item(b + 1, late_item)
                    else:
                        front(b, FRONT_B[s], last)
                    if i < NT or (s < NT and not last):
                        mean_variance(i % NT)
                scale_ffn(b, NT - 1)
                if last:
                    i = NT - 1
                    dve.wait_ge(y_scaled, NT * b + i + 1)
                    nc.vector.tensor_tensor(y[:, i % 4, :], y[:, i % 4, :], z[:, i % 4, :], ALU.add).then_inc(last_y_done, 1)

            nc.vector.memset(mean_scales[:, 0:1], -1.0 / D)
            nc.vector.memset(mean_scales[:, 1:2], 2.0 / D)
            nc.vector.memset(ones[:], 1.0).then_inc(ones_done, 1)
            for n in range(NC):
                split_kt(0, n)
            dve.wait_ge(const_in, CONSTS)
            nc.vector.tensor_copy(ident_b[:], ident[:]).then_inc(ident_b_done, 1)

            def first_statistics(i):
                dve.wait_ge(x_in_sem[i], 16)
                nc.vector.bn_stats(bn[:, i, :], x_raw[:, i, :]).then_inc(bn_done, 1)
                dve.wait_ge(bn_done, i + 1)
                mean_variance(i)

            def below(k):
                at = slice(k, k + 1)
                dve.wait_ge(w_abs_done, k + 1)
                nc.vector.tensor_scalar(w_scale[:, at], w_abs[:, at], 1.0 / D, QMIN, ALU.mult, ALU.max).then_inc(w_scale_done, 1)
                dve.wait_ge(w_scale_done, k + 1)
                nc.vector.tensor_scalar(w_nthr[:, at], w_scale[:, at], -0.5, None, ALU.mult).then_inc(w_thr_done, 1)
                nc.vector.tensor_scalar(w_thr[:, at], w_scale[:, at], 0.5, None, ALU.mult).then_inc(w_thr_done, 1)
                dve.wait_ge(w_thr_done, 2 * k + 2)
                nc.vector.tensor_scalar(w_below[:, k, :], w_raw[:, k, :], w_nthr[:, at], None, ALU.is_lt).then_inc(w_below_done, 1)

            def ternary(k):
                dve.wait_ge(w_below_done, k + 1)
                nc.vector.scalar_tensor_tensor(out=w_tern[:, k, :], in0=w_raw[:, k, :], scalar=w_thr[:, k:k + 1],
                                               in1=w_below[:, k, :], op0=ALU.is_gt, op1=ALU.subtract).then_inc(w_tern_done, 1)

            first_statistics(0)
            below(0)
            values(0, 0)
            ternary(0)
            mask_item(0, 0)
            below(1)
            split_item(0, 0)
            split_kt(0, NU - 2)
            mask_item(0, 1)
            split_kt(0, NU - 1)
            split_item(0, 1)
            mask_item(0, 2)
            below(2)
            split_item(0, 2)
            ternary(1)
            ternary(2)
            below(3)
            mask_item(0, 3)
            ternary(3)
            split_item(0, 3)
            first_statistics(1)
            item(0, 4)
            values(0, 1)
            first_statistics(2)
            first_statistics(3)
            with dve.Fori(0, B - 1) as b:
                batch(b, False)
            batch(B - 1, True)

        @block.gpsimd
        def _(pool):
            def norm(b, i):
                at = slice(i, i + 1)
                pool.wait_ge(mv_done, NT * b + i + 1)
                nc.gpsimd.tensor_tensor(var_eps[:, at], mv[:, i, 1:2], eps[:, 0:1], ALU.add).then_inc(var_eps_done, 1)
                pool.wait_ge(var_eps_done, NT * b + i + 1)
                nc.gpsimd.tensor_tensor(rstd[:, at], var_eps[:, at], minus_half[:], ALU.pow).then_inc(rstd_done, 1)

            def values_lo(b, i):
                pool.wait_ge(q_hi_done, NT * b + i + 1)
                nc.gpsimd.tensor_tensor(q_lo[:, i, :], q_full[:, i % 2, :], f32(q_hi[:, i, :]),
                                        ALU.subtract).then_inc(q_lo_done, 1)

            def split_kt(b, n):
                c, rows = unit(n)
                pool.wait_ge(kt_hi_done, NU * b + n + 1)
                nc.gpsimd.tensor_tensor(kt_lo[:, c, rows], kt_raw[:, c, rows], f32(kt_hi[:, c, rows]),
                                        ALU.subtract).then_inc(kt_lo_done[n // NC], 1)

            def x_sum(b, i):
                pool.wait_ge(q_done, NT * b + i + 1)
                nc.gpsimd.tensor_tensor(x_raw[:, i, :], x_raw[:, i, :], q_full[:, i % 2, :], ALU.add).then_inc(x_sum_done, 1)

            def upper_half(b, i):
                pool.wait_ge(z_done, NT * b + i + 1)
                nc.gpsimd.tensor_tensor(u[:, i % 2, HD:D], z[:, i % 4, 0:HD], z[:, i % 4, HD:D],
                                        ALU.subtract).then_inc(upper_done, 1)

            def norm_z(b, i):
                at = slice(i, i + 1)
                pool.wait_ge(sq_done, NT * b + i + 1)
                nc.gpsimd.tensor_tensor(z_sq_eps[:, at], z_sq[:, at], eps[:, 1:2], ALU.add).then_inc(z_eps_done, 1)
                pool.wait_ge(z_eps_done, NT * b + i + 1)
                nc.gpsimd.tensor_tensor(z_rstd[:, at], z_sq_eps[:, at], minus_half[:], ALU.pow).then_inc(z_rstd_done, 1)

            def add_z(b, i):
                pool.wait_ge(y_scaled, NT * b + i + 1)
                nc.gpsimd.tensor_tensor(y[:, i % 4, :], y[:, i % 4, :], z[:, i % 4, :], ALU.add).then_inc(y_done, 1)

            def batch(b, last):
                for s in range(SLOTS):
                    if s + AHEAD < NT:
                        norm(b, s + AHEAD)
                    if s >= NT and not last:
                        norm(b + 1, s - NT)
                    if s + 1 < NT:
                        values_lo(b, s + 1)
                        x_sum(b, s + 1)
                    if s == SLOTS - 1 and not last:
                        values_lo(b + 1, 0)
                        x_sum(b + 1, 0)
                    if s and not last:
                        for n in UNITS[s - 1]:
                            if n in POOL_UNITS:
                                split_kt(b + 1, n)
                    if s >= 3:
                        add_z(b, s - 3)
                    if s < NT:
                        upper_half(b, s)
                        norm_z(b, s)
                if not last:
                    add_z(b, NT - 1)

            nc.gpsimd.memset(minus_half[:], -0.5).then_inc(pool_const, 1)
            nc.gpsimd.memset(round_up[:], ROUND).then_inc(pool_const, 1)
            nc.gpsimd.memset(eps[:, 0:1], EPS).then_inc(pool_const, 1)
            nc.gpsimd.memset(eps[:, 1:2], D * EPS).then_inc(pool_const, 1)
            pool.wait_ge(pool_const, 4)
            norm(0, 0)
            for n in POOL_UNITS:
                split_kt(0, n)
            values_lo(0, 0)
            x_sum(0, 0)
            norm(0, 1)
            with pool.Fori(0, B - 1) as b:
                batch(b, False)
            batch(B - 1, True)


def kernel(x, ctx_1024, L0_ffn_weight):
    import numpy as np
    import concourse.bacc as bacc
    from concourse import mybir as mb
    from concourse.bass_utils import run_bass_kernel_spmd

    had = np.ones((1, 1), np.float32)
    while had.shape[0] < P:
        had = np.block([[had, had], [had, -had]])
    arrays = {
        "x_dram": np.ascontiguousarray(x),
        "ctx_dram": np.ascontiguousarray(np.transpose(ctx_1024, (0, 2, 1))),
        "weight_dram": np.ascontiguousarray(L0_ffn_weight),
        "ident_dram": np.eye(P, dtype=np.float32),
        "had_dram": np.ascontiguousarray(had, dtype=np.float32),
        "mask_dram": np.triu(np.ones((P, P), np.float32)),
    }
    nc = bacc.Bacc("TRN2", target_bir_lowering=False, num_devices=1)
    args = [nc.dram_tensor(n, a.shape, mb.dt.from_np(a.dtype), kind="ExternalInput").ap() for n, a in arrays.items()]
    out = nc.dram_tensor("out_dram", (B, L, D), mb.dt.float32, kind="ExternalOutput").ap()
    build(nc, *args, out)
    r = run_bass_kernel_spmd(nc, [arrays], core_ids=[0])
    return r.results[0]["out_dram"]
```
